# Optimizing a Trainium2 kernel written in Bass

```python
import numpy as np
import jax
import jax.numpy as jnp

def _softmax(x, axis=-1):
    return jax.nn.softmax(x, axis=axis)

def _gelu(x):
    return jax.nn.gelu(x, approximate=True)

def _silu(x):
    return jax.nn.silu(x)

def _sigmoid(x):
    return jax.nn.sigmoid(x)

def _layernorm(x, axis=-1, eps=1e-05):
    m = jnp.mean(x, axis=axis, keepdims=True)
    v = jnp.var(x, axis=axis, keepdims=True)
    return (x - m) / jnp.sqrt(v + eps)

def _scatter_add(tgt, idx, src, axis=0):
    return tgt.at[idx].add(src)

def _segment_sum(src, seg, n):
    return jax.ops.segment_sum(src, seg, n)
kernel_name = 'mk_adj_resnorm_d2_adj_r2_33b779'

def setup_inputs(seed: int=0):
    np.random.seed(seed)
    _w = jnp.asarray

    def _rec_inputs():
        import jax
        import jax.numpy as jnp
        _gk = jax.random.key(seed)
        x = 7.22e-05 + 1 * jax.random.normal(jax.random.fold_in(_gk, 1), (64, 128, 512), jnp.float32)
        _w = (1.0 + jnp.arange(128, dtype=jnp.float32)) ** (-0.5)
        _w = _w / _w.mean()
        _pij = jnp.clip(0.125 * _w[:, None] * _w[None, :], 0.0, 1.0)
        _a = jax.random.uniform(jax.random.fold_in(_gk, 2), (128, 128)) < _pij
        _a = jnp.logical_or(_a, jnp.swapaxes(_a, -1, -2))
        _a = jnp.logical_or(_a, jnp.eye(128, dtype=bool))
        _af = _a.astype(jnp.float32)
        _af = _af * jax.random.uniform(jax.random.fold_in(_gk, 3), (128, 128), jnp.float32, 0.05, 0.108252)
        adj = _af
        return (x, adj)
    x, adj = _rec_inputs()

    def _L0_gnn_setup():
        import jax, jax.numpy as jnp
        import numpy as np

        def _ada_gcn(xn, weight, bias):
            N, B, L = xn.shape
            x_norm = xn / jnp.maximum(jnp.linalg.norm(xn, axis=-1, keepdims=True), 1e-12)
            mean_sim = jnp.einsum('nbl,mbl->nm', x_norm, x_norm) / B
            k = max(int(N * 0.3), 1)
            _, idx = jax.lax.top_k(mean_sim, k + 1)
            rows = jnp.arange(N)[:, None]
            non_self = idx != rows
            order = jnp.cumsum(non_self.astype(jnp.int32), axis=1) - 1
            keep = non_self & (order < k)
            mask = jnp.zeros((N, N), dtype=bool).at[jnp.broadcast_to(rows, idx.shape), idx].set(keep)
            A = jnp.where(mask, mean_sim, jnp.zeros((), mean_sim.dtype))
            deg = A.sum(axis=0)
            dinv = jnp.where(deg > 0, jax.lax.rsqrt(deg), jnp.zeros((), deg.dtype))
            An = dinv[:, None] * A * dinv[None, :]
            xw = jnp.einsum('nbl,lo->nbo', xn, weight)
            out = jnp.einsum('sd,sbl->dbl', An, xw) + bias
            return out
        key = jax.random.key(seed)
        k1, k2 = jax.random.split(key)
        B, L, N = (32, 128, 512)
        x = jax.random.normal(k1, (B, L, N), dtype=jnp.float32)
        limit = float(np.sqrt(6.0 / (L + L)))
        weight = jax.random.uniform(k2, (L, L), dtype=jnp.float32, minval=-limit, maxval=limit)
        bias = jnp.zeros((L,), dtype=jnp.float32)
        return {'x': x, 'weight': weight, 'bias': bias}
    _L0_gnn_all = _L0_gnn_setup()
    _L0_gnn_in = {k: v for k, v in _L0_gnn_all.items() if k in ('bias',)}
    del _L0_gnn_all

    def _L1_gnn_setup():
        import jax, jax.numpy as jnp
        import numpy as np
        EPS = 1e-08

        def _row_stochastic_causal(A, causal_mask):
            A = A * causal_mask
            deg = jnp.maximum(A.sum(axis=-1, keepdims=True), EPS)
            return A / deg
        key = jax.random.key(seed)
        k = jax.random.split(key, 5)
        B, N, D = (4, 1024, 512)
        s = 1.0 / np.sqrt(D)
        h = jax.random.normal(k[0], (B, N, D), dtype=jnp.float32)
        W_lang = jax.random.normal(k[1], (D, D), dtype=jnp.float32) * s
        W_grav = jax.random.normal(k[2], (D, D), dtype=jnp.float32) * s
        W_V = jax.random.normal(k[3], (D, D), dtype=jnp.float32) * s
        W_O = jax.random.normal(k[4], (D, D), dtype=jnp.float32) * s
        causal_mask = jnp.tril(jnp.ones((N, N), dtype=jnp.float32))
        gate_logit = jnp.zeros((), jnp.float32)
        log_sigma = jnp.zeros((), jnp.float32)
        return {'h': h, 'causal_mask': causal_mask, 'W_lang': W_lang, 'W_grav': W_grav, 'W_V': W_V, 'W_O': W_O, 'gate_logit': gate_logit, 'log_sigma': log_sigma}
    _L1_gnn_all = _L1_gnn_setup()
    _L1_gnn_in = {k: v for k, v in _L1_gnn_all.items() if k in ('W_lang', 'W_grav', 'W_V', 'W_O', 'gate_logit', 'log_sigma')}
    del _L1_gnn_all
    return {'x': x, 'adj': adj, 'L0_gnn_bias': _L0_gnn_in['bias'], 'L1_gnn_W_lang': _L1_gnn_in['W_lang'], 'L1_gnn_W_grav': _L1_gnn_in['W_grav'], 'L1_gnn_W_V': _L1_gnn_in['W_V'], 'L1_gnn_W_O': _L1_gnn_in['W_O'], 'L1_gnn_gate_logit': _L1_gnn_in['gate_logit'], 'L1_gnn_log_sigma': _L1_gnn_in['log_sigma']}

def reference(x, adj, L0_gnn_bias, L1_gnn_W_lang, L1_gnn_W_grav, L1_gnn_W_V, L1_gnn_W_O, L1_gnn_gate_logit, L1_gnn_log_sigma):
    import jax
    import jax.numpy as jnp

    def _L0_gnn_ref(x, weight, bias):
        import jax, jax.numpy as jnp
        import numpy as np

        def _ada_gcn(xn, weight, bias):
            N, B, L = xn.shape
            x_norm = xn / jnp.maximum(jnp.linalg.norm(xn, axis=-1, keepdims=True), 1e-12)
            mean_sim = jnp.einsum('nbl,mbl->nm', x_norm, x_norm) / B
            k = max(int(N * 0.3), 1)
            _, idx = jax.lax.top_k(mean_sim, k + 1)
            rows = jnp.arange(N)[:, None]
            non_self = idx != rows
            order = jnp.cumsum(non_self.astype(jnp.int32), axis=1) - 1
            keep = non_self & (order < k)
            mask = jnp.zeros((N, N), dtype=bool).at[jnp.broadcast_to(rows, idx.shape), idx].set(keep)
            A = jnp.where(mask, mean_sim, jnp.zeros((), mean_sim.dtype))
            deg = A.sum(axis=0)
            dinv = jnp.where(deg > 0, jax.lax.rsqrt(deg), jnp.zeros((), deg.dtype))
            An = dinv[:, None] * A * dinv[None, :]
            xw = jnp.einsum('nbl,lo->nbo', xn, weight)
            out = jnp.einsum('sd,sbl->dbl', An, xw) + bias
            return out
        xn = jnp.transpose(x, (2, 0, 1))
        num_levels = 1
        for _ in range(num_levels):
            xn = _ada_gcn(xn, weight, bias)
        return jnp.transpose(xn, (1, 2, 0))

    def _L1_gnn_ref(h, causal_mask, W_lang, W_grav, W_V, W_O, gate_logit, log_sigma):
        import jax, jax.numpy as jnp
        import numpy as np
        EPS = 1e-08

        def _row_stochastic_causal(A, causal_mask):
            A = A * causal_mask
            deg = jnp.maximum(A.sum(axis=-1, keepdims=True), EPS)
            return A / deg
        z_l = jnp.einsum('bnd,ed->bne', h, W_lang)
        z_g = jnp.einsum('bnd,ed->bne', h, W_grav)
        v = jnp.einsum('bnd,ed->bne', h, W_V)
        N = h.shape[-2]
        not_eye = 1.0 - jnp.eye(N, dtype=h.dtype)
        zn = z_l / jnp.maximum(jnp.linalg.norm(z_l, axis=-1, keepdims=True), EPS)
        A_l = jnp.maximum(jnp.einsum('bnd,bmd->bnm', zn, zn), 0.0) * not_eye
        sq = jnp.sum(z_g * z_g, axis=-1, keepdims=True)
        d2 = jnp.maximum(sq + jnp.swapaxes(sq, -1, -2) - 2.0 * jnp.einsum('bnd,bmd->bnm', z_g, z_g), 0.0)
        sigma = jnp.exp(log_sigma)
        A_g = jnp.exp(-d2 / (2.0 * sigma * sigma)) * not_eye
        K_l = _row_stochastic_causal(A_l, causal_mask)
        K_g = _row_stochastic_causal(A_g, causal_mask)
        w_l = jax.nn.sigmoid(gate_logit)
        K = w_l * K_l + (1.0 - w_l) * K_g
        out = jnp.einsum('bnm,bmd->bnd', K, v)
        return jnp.einsum('bnd,ed->bne', out, W_O)
    x = _layernorm(x + _L0_gnn_ref(x, adj, L0_gnn_bias), axis=-1)
    x = _layernorm(x + _L1_gnn_ref(x, adj, L1_gnn_W_lang, L1_gnn_W_grav, L1_gnn_W_V, L1_gnn_W_O, L1_gnn_gate_logit, L1_gnn_log_sigma), axis=-1)
    return x

_drawn_inputs = setup_inputs


def setup_inputs(seed=0):
    import zlib

    import numpy as np

    out = dict(_drawn_inputs(seed))
    spreads = {'L0_gnn_bias': (0.0, 0.1)}
    factors = {}
    for name, (base, spread) in spreads.items():
        noise = np.random.default_rng([zlib.crc32(name.encode()), seed]).standard_normal(out[name].shape)
        drawn = base * np.exp(spread * noise) if base else spread * noise
        out[name] = jnp.asarray(drawn.astype(out[name].dtype))
    for name, factor in factors.items():
        out[name] = (out[name] * factor).astype(out[name].dtype)
    return out
```

```python
from contextlib import ExitStack

import concourse.bass as bass
from concourse import mybir

ALU = mybir.AluOpType
ACT = mybir.ActivationFunctionType
F32 = mybir.dt.float32
F32R = mybir.dt.float32r
AX = mybir.AxisListType.X

P = 128
B, L, N = 64, 128, 512
NT = N // P
TOPK = max(int(N * 0.3), 1)
ROUNDS = (TOPK + 7) // 8
DUMMIES = ROUNDS * 8 - TOPK
DUMMY, SELF, TAKEN = 1e30, -1e30, -3e38
NORM_EPS, KERNEL_EPS, LN_EPS = 1e-12, 1e-8, 1e-5
GROUP = 4
GROUPS = B // GROUP

CHUNK = 8
SLOTS = 2 * CHUNK
LEAD = 12
PASSES = B // SLOTS
SIM_FROM = [0, P, 2 * P, 2 * P]


def tile_cols(t):
    return slice(t * P, (t + 1) * P)


def constants(nc, sb, sem, adj, bias, gate, log_sigma):
    c = {
        "ident": sb("ident", [P, P], F32),
        "ones": sb("ones", [P, P], F32),
        "ones_r": sb("ones_r", [P, P], F32R),
        "adj": sb("adj_sb", [P, P], F32),
        "mask": sb("mask", [P, P], F32),
        "bias": sb("bias_sb", [P, 1], F32),
        "gate": sb("gate_sb", [P, 1], F32),
        "log_sigma": sb("log_sigma_sb", [P, 1], F32),
        "scal": sb("scal", [P, 8], F32),
        "eps": sb("eps", [P, 1], F32),
    }
    return c


def gated_graph_block(nc, x, adj, bias, w_lang, w_grav, w_v, w_o, gate, log_sigma, out):
    with ExitStack() as whole:
        def sb(name, shape, dt, scope=whole):
            return scope.enter_context(nc.sbuf_tensor(name, shape, dt))

        def sem(name, scope=whole):
            return scope.enter_context(nc.semaphore(name))

        c = constants(nc, sb, sem, adj, bias, gate, log_sigma)
        banks = [whole.enter_context(nc.psum_tensor(f"bank{n}", [P, 512], F32)) for n in range(8)]
        an_hi = sb("an_hi", [P, NT, N], F32R)
        an_lo = sb("an_lo", [P, NT, N], F32R)
        kept = {"an": (an_hi, an_lo)}
        for name in ("ml", "mg", "vo"):
            kept[name] = (sb(name + "_hi", [P, NT, N], F32R), sb(name + "_lo", [P, NT, N], F32R))

        with ExitStack() as early:
            raw = {n: sb("raw_" + n, [P, NT, N], F32, early) for n in ("l", "g", "v", "o")}
            weights_in = sem("weights_in")
            setup_block(nc, sem, sb, early, c, raw, weights_in, adj, bias, gate, log_sigma,
                        {"l": w_lang, "g": w_grav, "v": w_v, "o": w_o})
            similarity(nc, sb, sem, early, c, banks, x)
            graph_and_weights(nc, sb, sem, early, c, banks, raw, weights_in, kept)
        layers(nc, sb, sem, c, banks, kept, x, out)



def setup_block(nc, sem, sb, early, c, raw, weights_in, adj, bias, gate, log_sigma, weights):
    small_in, filled, cleared = sem("small_in"), sem("filled"), sem("cleared")
    exps, step = sem("exps"), sem("setup_step")
    wide = sb("wide", [P, CHUNK + P], F32, early)
    c["place"] = sb("place", [P, CHUNK + P], F32R, early)
    c["pick"] = sb("pick", [P, CHUNK, P], F32R, early)
    both = sb("both", [P, CHUNK], F32, early)
    scal = c["scal"]

    with nc.Block() as block:
        @block.sync
        def _(sp):
            sp.dma_start(c["adj"][:], adj).then_inc(small_in, 16)
            sp.dma_start(c["bias"][:], bias.rearrange("(p a) -> p a", a=1)).then_inc(small_in, 16)
            for name, source in (("gate", gate), ("log_sigma", log_sigma)):
                sp.dma_start(c[name][:], source.to_broadcast([P, 1])).then_inc(small_in, 16)
            for name in ("l", "g", "o", "v"):
                sp.dma_start(raw[name][:], weights[name].rearrange("(t p) d -> p t d", p=P)
                             ).then_inc(weights_in, 16)

        @block.gpsimd
        def _(pool):
            nc.gpsimd.memset(c["ident"][:], 0.0).then_inc(cleared, 1)
            nc.gpsimd.memset(wide[:], 0.0).then_inc(cleared, 1)
            nc.gpsimd.memset(c["ones"][:], 1.0).then_inc(filled, 1)
            nc.gpsimd.memset(c["eps"][:], LN_EPS).then_inc(filled, 1)
            pool.wait_ge(cleared, 2)
            nc.gpsimd.affine_select(out=c["ident"][:], in_=c["ident"][:], compare_op=ALU.not_equal,
                                    fill=1.0, base=0, pattern=[[-1, P]], channel_multiplier=1
                                    ).then_inc(filled, 1)
            nc.gpsimd.memset(wide[:, CHUNK - 1:CHUNK], 1.0).then_inc(filled, 1)
            nc.gpsimd.memset(wide[:, CHUNK + 63:CHUNK + 64], 1.0).then_inc(filled, 1)

        @block.scalar
        def _(act):
            act.wait_ge(small_in, 64)
            nc.scalar.activation(scal[:, 4:5], c["gate"][:], ACT.Exp, scale=-1.0).then_inc(exps, 1)
            nc.scalar.activation(scal[:, 5:6], c["log_sigma"][:], ACT.Exp).then_inc(exps, 1)

        @block.vector
        def _(dve):
            dve.wait_ge(filled, 5)
            nc.vector.tensor_copy(c["ones_r"][:], c["ones"][:])
            nc.vector.tensor_copy(c["place"][:], wide[:])
            nc.vector.tensor_tensor(both[:], c["ident"][:, 0:CHUNK], c["ident"][:, 64:64 + CHUNK],
                                    ALU.add).then_inc(step, 1)
            nc.vector.tensor_scalar(c["mask"][:], c["ident"][:], -1.0, 1.0, ALU.mult, ALU.add
                                    ).then_inc(step, 1)
            dve.wait_ge(step, 2)
            nc.vector.tensor_copy(c["pick"][:], both[:, :, None].to_broadcast([P, CHUNK, P]))
            dve.wait_ge(small_in, 64)
            nc.vector.tensor_tensor(c["mask"][:], c["mask"][:], c["adj"][:], ALU.mult).then_inc(step, 1)
            dve.wait_ge(exps, 2)
            nc.vector.tensor_scalar(scal[:, 6:7], scal[:, 4:5], 1.0, None, ALU.add).then_inc(step, 1)
            nc.vector.tensor_scalar(scal[:, 7:8], scal[:, 5:6], scal[:, 5:6], -2.0, ALU.mult, ALU.mult
                                    ).then_inc(step, 1)
            dve.wait_ge(step, 5)
            nc.vector.reciprocal(scal[:, 0:1], scal[:, 6:7]).then_inc(step, 1)
            nc.vector.reciprocal(scal[:, 2:3], scal[:, 7:8]).then_inc(step, 1)
            dve.wait_ge(step, 7)
            nc.vector.tensor_scalar(scal[:, 1:2], scal[:, 0:1], -1.0, 1.0, ALU.mult, ALU.add)



def similarity(nc, sb, sem, early, c, banks, x):
    with ExitStack() as scope:
        def buf(name, shape, dt):
            return sb(name, shape, dt, scope)

        x_ring = buf("x_ring", [P, SLOTS, N], F32)
        sq = buf("sq", [P, 2, N], F32)
        sq_hi = buf("sq_hi", [P, 2, N], F32R)
        sq_lo = buf("sq_lo", [P, 2, N], F32R)
        root = buf("root", [P, N], F32)
        inv = buf("inv", [P, N], F32)
        inv_split = buf("inv_split", [P, 2, N], F32R)
        xn = buf("xn", [P, 2, N], F32)
        xn_hi = buf("xn_hi", [P, 4, N], F32R)
        xn_lo = buf("xn_lo", [P, 4, N], F32R)
        sums, spread = banks[4:6], banks[6:8]

        x_in = [sem(f"x_in{s}") for s in range(SLOTS)]
        squared, squares_split, squares_used = sem("squared"), sem("squares_split"), sem("squares_used")
        roots_ready, clamped = sem("roots_ready"), sem("clamped")
        inverted, inv_hi_ready, inv_ready = sem("inverted"), sem("inv_hi_ready"), sem("inv_ready")
        spread_ready, scaled, hi_ready, lo_ready = (sem("spread_ready"), sem("scaled"), sem("hi_ready"),
                                                    sem("lo_ready"))
        grams_done = sem("grams_done")

        with nc.Block() as block:
            @block.sync
            def _(sp):
                for k in range(SLOTS):
                    sp.dma_start(x_ring[:, k, :], x[k]).then_inc(x_in[k], 16)
                with sp.Fori(0, PASSES - 1) as p:
                    for j in range(SLOTS):
                        sp.wait_ge(scaled, p * SLOTS + (j + 1))
                        sp.dma_start(x_ring[:, j, :],
                                     x[bass.ds(p * SLOTS + (SLOTS + j), 1)].rearrange("a l n -> l (a n)")
                                     ).then_inc(x_in[j], 16)

            @block.gpsimd
            def _(pool):
                def split(p, j, first=False):
                    pool.wait_ge(squared, p * SLOTS + (j + 1))
                    if not (first and j < 2):
                        pool.wait_ge(squares_used, p * SLOTS + (j - 1))
                    nc.gpsimd.tensor_tensor(sq_lo[:, j % 2, :], sq[:, j % 2, :], sq_hi[:, j % 2, :].bitcast(F32),
                                            ALU.subtract).then_inc(squares_split, 1)

                for k in range(LEAD):
                    split(0, k, first=True)
                with pool.Fori(0, PASSES - 1) as p:
                    for j in range(SLOTS):
                        split(p, j + LEAD)
                for j in range(SLOTS - LEAD):
                    split(PASSES - 1, j + LEAD)

            @block.scalar
            def _(act):
                def square(p, j, first=False):
                    act.wait_ge(x_in[j % SLOTS], (p + (1 + j // SLOTS)) * 16)
                    if not (first and j < 2):
                        act.wait_ge(squares_split, p * SLOTS + (j - 1))
                        act.wait_ge(squares_used, p * SLOTS + (j - 1))
                    nc.scalar.activation(sq[:, j % 2, :], x_ring[:, j % SLOTS, :], ACT.Square)
                    nc.scalar.activation(sq_hi[:, j % 2, :], x_ring[:, j % SLOTS, :], ACT.Square
                                         ).then_inc(squared, 1)

                def roots(p, chunk, first=False):
                    act.wait_ge(squares_used, p * SLOTS + (chunk + 1) * CHUNK)
                    if not (first and chunk == 0):
                        act.wait_ge(inverted, p * 2 * NT + chunk * NT)
                    nc.scalar.activation(root[:], sums[chunk % 2][:], ACT.Sqrt).then_inc(roots_ready, 1)

                def hi(p, j, first=False):
                    act.wait_ge(scaled, p * SLOTS + (j + 1))
                    if not (first and j < 4):
                        act.wait_ge(grams_done, p * SLOTS + (j - 3))
                    nc.scalar.activation(xn_hi[:, j % 4, :], xn[:, j % 2, :], ACT.Copy).then_inc(hi_ready, 1)

                for k in range(LEAD):
                    square(0, k, first=True)
                    if k == CHUNK:
                        roots(0, 0, first=True)

                def one_pass(p, last=False, first=False):
                    for j in range(SLOTS):
                        if not last or j + LEAD < SLOTS:
                            square(p, j + LEAD)
                        if j == 4:
                            roots(p, 1)
                        if j == 12 and not last:
                            roots(p, 2)
                        hi(p, j, first)

                one_pass(0, first=True)
                with act.Fori(1, PASSES - 1) as p:
                    one_pass(p)
                one_pass(PASSES - 1, last=True)

            @block.vector
            def _(dve):
                def clamp(p, chunk):
                    dve.wait_ge(roots_ready, p * 2 + (chunk + 1))
                    nc.vector.tensor_scalar(root[:], root[:], NORM_EPS, None, ALU.max).then_inc(clamped, 1)

                def invert(p, chunk, t):
                    if t == 0:
                        dve.wait_ge(clamped, p * 2 + (chunk + 1))
                    nc.vector.reciprocal(inv[:, tile_cols(t)], root[:, tile_cols(t)]).then_inc(inverted, 1)

                def split_inverse(p, chunk, first=False):
                    side = chunk % 2
                    dve.wait_ge(inverted, p * 2 * NT + (chunk + 1) * NT)
                    if not (first and chunk < 2):
                        dve.wait_ge(spread_ready, p * SLOTS + (chunk - 1) * CHUNK)
                    nc.vector.tensor_copy(inv_split[:, side, :], inv[:]).then_inc(inv_hi_ready, 1)
                    dve.wait_ge(inv_hi_ready, p * 2 + (chunk + 1))
                    nc.vector.tensor_tensor(inv_split[64:P, side, :], inv[64:P, :],
                                            inv_split[64:P, side, :].bitcast(F32), ALU.subtract).then_inc(inv_ready, 1)

                def scale(p, j, first=False):
                    dve.wait_ge(spread_ready, p * SLOTS + (j + 1))
                    nc.vector.tensor_tensor(xn[:, j % 2, :], x_ring[:, j % SLOTS, :], spread[j % 2][:],
                                            ALU.mult).then_inc(scaled, 1)

                def lo(p, j, first=False):
                    dve.wait_ge(hi_ready, p * SLOTS + (j + 1))
                    nc.vector.tensor_tensor(xn_lo[:, j % 4, :], xn[:, j % 2, :], xn_hi[:, j % 4, :].bitcast(F32),
                                            ALU.subtract).then_inc(lo_ready, 1)

                clamp(0, 0)
                for t in range(NT):
                    invert(0, 0, t)
                split_inverse(0, 0, first=True)

                def one_pass(p, last=False, first=False):
                    for j in range(SLOTS):
                        if not (first and j == 0):
                            if j == 0:
                                lo(p - 1, SLOTS - 1)
                            else:
                                lo(p, j - 1)
                        scale(p, j, first)
                        for at, chunk in ((4, 1), (12, 2)):
                            if chunk == 2 and last:
                                continue
                            if j == at:
                                clamp(p, chunk)
                                invert(p, chunk, 0)
                            if j == at + 1:
                                invert(p, chunk, 1)
                                invert(p, chunk, 2)
                            if j == at + 2:
                                invert(p, chunk, 3)
                                split_inverse(p, chunk, first)

                one_pass(0, first=True)
                with dve.Fori(1, PASSES - 1) as p:
                    one_pass(p)
                one_pass(PASSES - 1, last=True)
                lo(PASSES - 1, SLOTS - 1)

            @block.tensor
            def _(pe):
                def sum_squares(p, j, first=False):
                    side = banks[4 + (j // CHUNK) % 2]
                    b = j % CHUNK
                    where = c["place"][:, CHUNK - 1 - b:CHUNK - 1 - b + P]
                    pe.wait_ge(squares_split, p * SLOTS + (j + 1))
                    if b == 0 and not (first and j < SLOTS):
                        pe.wait_ge(roots_ready, p * 2 + (j // CHUNK - 1))
                    nc.tensor.matmul(side[:], where, sq_hi[:, j % 2, :], start=(b == 0), stop=False)
                    last = nc.tensor.matmul(side[:], where, sq_lo[:, j % 2, :], start=False,
                                            stop=(b == CHUNK - 1))
                    last.then_inc(squares_used, 1)
                    return last

                def spread_inverse(p, j, first=False):
                    if j % CHUNK == 0:
                        pe.wait_ge(inv_ready, p * 2 + (j // CHUNK + 1))
                    if not (first and j < 2):
                        pe.wait_ge(scaled, p * SLOTS + (j - 1))
                    nc.tensor.matmul(spread[j % 2][:], c["pick"][:, j % CHUNK, :],
                                     inv_split[:, (j // CHUNK) % 2, :], start=True, stop=True
                                     ).then_inc(spread_ready, 1)

                def gram(p, j, start=False, stop=False):
                    pe.wait_ge(lo_ready, p * SLOTS + (j + 1))
                    h, l = xn_hi[:, j % 4, :], xn_lo[:, j % 4, :]
                    for n, (left, right) in enumerate(((h, h), (h, l), (l, h))):
                        for t in range(NT):
                            last = nc.tensor.matmul(banks[t][:, 0:N - SIM_FROM[t]], left[:, tile_cols(t)],
                                                    right[:, SIM_FROM[t]:N], start=(start and n == 0),
                                                    stop=(stop and n == 2))
                    last.then_inc(grams_done, 1)

                for k in range(LEAD):
                    sum_squares(0, k, first=True)
                spread_inverse(0, 0, first=True)

                def one_pass(p, first=False, last=False):
                    for j in range(SLOTS):
                        if not last or j + LEAD < SLOTS:
                            sum_squares(p, j + LEAD, first)
                        if not last or j + 1 < SLOTS:
                            spread_inverse(p, j + 1, first)
                        gram(p, j, start=(first and j == 0), stop=(last and j == SLOTS - 1))

                one_pass(0, first=True)
                with pe.Fori(1, PASSES - 1) as p:
                    one_pass(p)
                one_pass(PASSES - 1, last=True)



def graph_and_weights(nc, sb, sem, early, c, banks, raw, weights_in, kept):
    with ExitStack() as scope:
        def buf(name, shape, dt):
            return sb(name, shape, dt, scope)

        sim = buf("sim", [P, NT, N], F32)
        work = buf("work", [P, NT, N + DUMMIES], F32)
        top8 = buf("top8", [P, NT, 8], F32)
        graph = buf("graph", [P, NT, N], F32)
        wo_t = buf("wo_t", [P, NT, N], F32)
        full = buf("full", [P, 2, N], F32)
        diag = buf("diag", [P, NT, P], F32)
        deg = buf("deg", [P, 5, NT], F32)
        an = buf("an", [P, 2, N], F32)
        an_hi, an_lo = kept["an"]
        degree_bank, mirror_banks, dinv_bank = banks[7], banks[4:7], banks[4]
        ident4 = c["ident"][:, None, :].to_broadcast([P, NT, P])

        sim_upper, mirrored, sim_ready = sem("sim_upper"), sem("mirrored"), sem("sim_ready")
        work_ready, top8_ready, graph_ready = sem("work_ready"), sem("top8_ready"), sem("graph_ready")
        product_ready, product_read, product_split = (sem("product_ready"), sem("product_read"),
                                                      sem("product_split"))
        degree_spread, degree_step, degree_root = sem("degree_spread"), sem("degree_step"), sem("degree_root")
        dinv_spread, an_ready, an_hi_ready, an_read = (sem("dinv_spread"), sem("an_ready"),
                                                       sem("an_hi_ready"), sem("an_read"))

        products = ([("ml", t) for t in range(NT)] + [("mg", t) for t in range(NT)]
                    + [("wo_t", t) for t in range(NT)] + [("vo", t) for t in range(NT)])
        width = {kind: [N] * NT for kind in ("wo_t", "vo")}
        width["ml"] = width["mg"] = [(t + 1) * P for t in range(NT)]
        split_products = [n for n, (kind, _) in enumerate(products) if kind != "wo_t"]

        with nc.Block() as block:
            @block.tensor
            def _(pe):
                for rows, bank in ((1, 0), (2, 1), (3, 2)):
                    pe.wait_ge(sim_upper, min(rows, 2))
                    for t in range(min(rows, 2)):
                        last = nc.tensor.transpose(mirror_banks[bank][:, tile_cols(t)],
                                                   sim[:, t, tile_cols(rows)], c["ident"][:])
                    last.then_inc(mirrored, 1)
                pe.wait_ge(weights_in, 64)
                pe.wait_ge(sim_upper, NT)
                for n, (kind, t) in enumerate(products):
                    bank = banks[n % 4]
                    if n >= 4:
                        pe.wait_ge(product_read, n - 3)
                    if (kind, t) == ("vo", 0):
                        pe.wait_ge(product_read, n)
                    for k in range(NT):
                        if kind == "wo_t":
                            last = nc.tensor.transpose(bank[:, tile_cols(k)], raw["o"][:, k, tile_cols(t)],
                                                       c["ident"][:])
                        elif kind == "vo":
                            last = nc.tensor.matmul(bank[:], raw["v"][:, k, tile_cols(t)], wo_t[:, k, :],
                                                    start=(k == 0), stop=(k == NT - 1))
                        else:
                            w = raw[kind[1]]
                            last = nc.tensor.matmul(bank[:, 0:width[kind][t]], w[:, k, tile_cols(t)],
                                                    w[:, k, 0:width[kind][t]], start=(k == 0),
                                                    stop=(k == NT - 1))
                    last.then_inc(product_ready, 1)
                for t in range(NT):
                    pe.wait_ge(graph_ready, t + 1)
                    last = nc.tensor.matmul(degree_bank[:], c["ones"][:], graph[:, t, :],
                                            start=(t == 0), stop=(t == NT - 1))
                last.then_inc(degree_spread, 1)
                pe.wait_ge(degree_step, 7)
                nc.tensor.matmul(dinv_bank[:], c["ones"][:], diag[:], start=True, stop=True
                                 ).then_inc(dinv_spread, 1)

            @block.scalar
            def _(act):
                for t in range(NT):
                    nc.scalar.activation(sim[:, t, SIM_FROM[t]:N], banks[t][:, 0:N - SIM_FROM[t]],
                                         ACT.Copy, scale=1.0 / B).then_inc(sim_upper, 1)
                for rows, bank in ((1, 0), (2, 1), (3, 2)):
                    act.wait_ge(mirrored, rows)
                    w = min(rows, 2) * P
                    nc.scalar.activation(sim[:, rows, 0:w], mirror_banks[bank][:, 0:w], ACT.Copy
                                         ).then_inc(sim_ready, 1)
                for n, (kind, t) in enumerate(products):
                    bank, w = banks[n % 4], width[kind][t]
                    act.wait_ge(product_ready, n + 1)
                    if kind == "wo_t":
                        nc.scalar.activation(wo_t[:, t, :], bank[:], ACT.Copy).then_inc(product_read, 1)
                        continue
                    m = split_products.index(n)
                    if m >= 2:
                        act.wait_ge(product_split, m - 1)
                    parts = [(0, w, 1.0)] if kind == "vo" else [(0, w - P, 1.0), (w - P, w, 0.5)]
                    for a, b, scale in parts:
                        if a == b:
                            continue
                        nc.scalar.activation(full[:, m % 2, a:b], bank[:, a:b], ACT.Copy, scale=scale)
                        last = nc.scalar.activation(kept[kind][0][:, t, a:b], bank[:, a:b], ACT.Copy,
                                                    scale=scale)
                    last.then_inc(product_read, 1)
                act.wait_ge(degree_step, 3)
                nc.scalar.activation(deg[:, 2, :], deg[:, 1, :], ACT.Sqrt).then_inc(degree_root, 1)
                for t in range(NT):
                    act.wait_ge(an_ready, t + 1)
                    nc.scalar.activation(an_hi[:, t, :], an[:, t % 2, :], ACT.Copy).then_inc(an_hi_ready, 1)

            @block.gpsimd
            def _(pool):
                for m, n in enumerate(split_products):
                    kind, t = products[n]
                    w = width[kind][t]
                    pool.wait_ge(product_read, n + 1)
                    nc.gpsimd.tensor_tensor(kept[kind][1][:, t, 0:w], full[:, m % 2, 0:w],
                                            kept[kind][0][:, t, 0:w].bitcast(F32), ALU.subtract
                                            ).then_inc(product_split, 1)

            @block.vector
            def _(dve):
                nc.vector.memset(work[:, :, N:N + DUMMIES], DUMMY)
                for t in range(NT):
                    if t == 0:
                        dve.wait_ge(sim_upper, 1)
                    else:
                        dve.wait_ge(sim_ready, t)
                    nc.vector.tensor_copy(work[:, t, 0:N], sim[:, t, :]).then_inc(top8_ready, 1)
                for t in range(NT):
                    dve.wait_ge(top8_ready, t + 1)
                    nc.vector.scalar_tensor_tensor(out=work[:, t, tile_cols(t)], in0=c["ident"][:],
                                                   scalar=SELF, in1=sim[:, t, tile_cols(t)],
                                                   op0=ALU.mult, op1=ALU.add).then_inc(work_ready, 1)
                with dve.Fori(0, ROUNDS) as r:
                    for t in range(NT):
                        dve.wait_ge(work_ready, r * NT + (t + 1))
                        dve.nop(nofuse=True)
                        nc.vector.max(top8[:, t, :], work[:, t, :]).then_inc(top8_ready, 1)
                    for t in range(NT):
                        dve.wait_ge(top8_ready, r * NT + (NT + t + 1))
                        dve.nop(nofuse=True)
                        nc.vector.match_replace(work[:, t, :], top8[:, t, :], work[:, t, :], TAKEN
                                                ).then_inc(work_ready, 1)
                for t in range(NT):
                    dve.wait_ge(work_ready, ROUNDS * NT + t + 1)
                    nc.vector.scalar_tensor_tensor(out=graph[:, t, :], in0=work[:, t, 0:N], scalar=TAKEN,
                                                   in1=sim[:, t, :], op0=ALU.is_equal, op1=ALU.mult
                                                   ).then_inc(graph_ready, 1)
                dve.wait_ge(degree_spread, 1)
                nc.vector.tensor_tensor(diag[:], degree_bank[:].rearrange("p (t m) -> p t m", t=NT),
                                        ident4, ALU.mult).then_inc(degree_step, 1)
                dve.wait_ge(degree_step, 1)
                nc.vector.tensor_reduce(deg[:, 0, :], diag[:], AX, ALU.add).then_inc(degree_step, 1)
                dve.wait_ge(degree_step, 2)
                nc.vector.tensor_scalar(deg[:, 1, :], deg[:, 0, :], 1.2e-38, None, ALU.max
                                        ).then_inc(degree_step, 1)
                nc.vector.tensor_scalar(deg[:, 3, :], deg[:, 0, :], 0.0, None, ALU.is_gt
                                        ).then_inc(degree_step, 1)
                dve.wait_ge(degree_root, 1)
                nc.vector.reciprocal(deg[:, 2, :], deg[:, 2, :]).then_inc(degree_step, 1)
                dve.wait_ge(degree_step, 5)
                nc.vector.tensor_tensor(deg[:, 4, :], deg[:, 2, :], deg[:, 3, :], ALU.mult
                                        ).then_inc(degree_step, 1)
                dve.wait_ge(degree_step, 6)
                nc.vector.tensor_tensor(diag[:], ident4, deg[:, 4, :, None].to_broadcast([P, NT, P]),
                                        ALU.mult).then_inc(degree_step, 1)
                dve.wait_ge(dinv_spread, 1)

                def split_an(t):
                    dve.wait_ge(an_hi_ready, t + 1)
                    nc.vector.tensor_tensor(an_lo[:, t, :], an[:, t % 2, :], an_hi[:, t, :].bitcast(F32), ALU.subtract
                                            ).then_inc(an_read, 1)

                for t in range(NT):
                    if t >= 2:
                        dve.wait_ge(an_read, t - 1)
                    nc.vector.scalar_tensor_tensor(out=an[:, t % 2, :], in0=graph[:, t, :],
                                                   scalar=deg[:, 4, t:t + 1], in1=dinv_bank[:],
                                                   op0=ALU.mult, op1=ALU.mult).then_inc(an_ready, 1)
                    if t:
                        split_an(t - 1)
                split_an(NT - 1)



RING = 4
FRONT_USES = ([("xw", b) for b in range(GROUP)] + [("mix", b) for b in range(GROUP)]
              + [("h_t", b) for b in range(GROUP)])
LOOP_USES = ([("t_l", t) for t in range(NT)] + [("t_g", t) for t in range(NT)]
             + [("v", b) for b in range(GROUP)]
             + [("xw", b) for b in range(GROUP)] + [("mix", b) for b in range(GROUP)]
             + [("h_t", 0), ("h_t", 1), ("h_t", 2), ("kv", 0), ("kv", 1), ("h_t", 3), ("kv", 2), ("kv", 3)])
BACK_USES = ([("t_l", t) for t in range(NT)] + [("t_g", t) for t in range(NT)]
             + [("v", b) for b in range(GROUP)] + [("kv", b) for b in range(GROUP)])
assert len(FRONT_USES) % RING == len(LOOP_USES) % RING == len(BACK_USES) % RING == 0


def ring_use(when, i, use):
    uses = {"front": FRONT_USES, "loop": LOOP_USES, "back": BACK_USES}[when]
    at = uses.index(use)
    if when == "front":
        return at % RING, at // RING
    return at % RING, i * (len(LOOP_USES) // RING) + (len(FRONT_USES) // RING + at // RING)


def layers(nc, sb, sem, c, banks, kept, x, out):
    with ExitStack() as scope:
        def buf(name, shape, dt):
            return sb(name, shape, dt, scope)

        x_sb = buf("x_sb", [P, GROUP, N], F32)
        xw_hi, xw_lo = (buf(n, [P, GROUP, NT, P], F32R) for n in ("xw_hi", "xw_lo"))
        y = buf("y", [P, 2, N], F32)
        h = buf("h", [P, GROUP, N], F32)
        h_kept = buf("h_kept", [P, GROUP, N], F32)
        ht = buf("ht", [P, NT, GROUP, P], F32)
        ht_hi, ht_lo = (buf(n, [P, NT, GROUP, P], F32R) for n in ("ht_hi", "ht_lo"))
        t_mat = {"l": buf("t_l", [P, NT, GROUP, P], F32), "g": buf("t_g", [P, NT, GROUP, P], F32)}
        v_hi, v_lo = (buf(n, [P, GROUP, N], F32R) for n in ("v_hi", "v_lo"))
        p_mat = {m: buf("p_" + m, [P, GROUP, P], F32) for m in "lg"}
        g_mat = {m: buf("g_" + m, [P, GROUP, P], F32) for m in "lg"}
        on_diag = {m: buf("on_diag_" + m, [P, GROUP, P], F32) for m in "lg"}
        d_hi = {m: buf("d_hi_" + m, [P, GROUP, P], F32R) for m in "lg"}
        d_lo = {m: buf("d_lo_" + m, [P, GROUP, P], F32R) for m in "lg"}
        kern = {m: buf("kern_" + m, [P, GROUP, P], F32) for m in "lg"}
        masked = {m: on_diag[m] for m in "lg"}
        k_mat = buf("k_mat", [P, GROUP, P], F32)
        kt_hi, kt_lo = (buf(n, [P, GROUP, P], F32R) for n in ("kt_hi", "kt_lo"))
        y2 = buf("y2", [P, 2, N], F32)
        o_sb = buf("o_sb", [P, 2, N], F32)
        stats = buf("stats", [P, 2, 2, 6], F32)
        moments = buf("moments", [P, 2, 2, 2], F32)
        sd = buf("sd", [P, 2, 2, 2], F32)
        sq = {m: buf("sq_" + m, [P, GROUP], F32) for m in "lg"}
        norm = buf("norm", [P, 3, GROUP], F32)
        small_hi = {m: buf("small_hi_" + m, [P, GROUP], F32R) for m in "lg"}
        small_lo = {m: buf("small_lo_" + m, [P, GROUP], F32R) for m in "lg"}
        row = {m: buf("row_" + m, [P, 4, GROUP], F32) for m in "lg"}
        (ml, mg, vo), (an_hi, an_lo) = (kept[n] for n in ("ml", "mg", "vo")), kept["an"]
        scal = c["scal"]
        every_ident = c["ident"][:, None, :].to_broadcast([P, GROUP, P])
        every_mask = c["mask"][:, None, :].to_broadcast([P, GROUP, P])

        def each(small):
            return small[:, :, None].to_broadcast([P, GROUP, P])

        def flat(t):
            return t[:].rearrange("p b m -> p (b m)")

        gram_bank = {"l": banks[4], "g": banks[5]}
        mirror_bank = {"l": banks[6], "g": banks[7]}
        spread_bank = gram_bank
        kt_bank = banks[6]

        ring_full = [sem(f"ring_full{r}") for r in range(RING)]
        ring_read = [sem(f"ring_read{r}") for r in range(RING)]
        x_in = [sem(f"xb_in{b}") for b in range(GROUP)]
        o_free = [sem(f"o_free{s}") for s in range(2)]
        xw_hi_ready, v_hi_ready, ht_hi_ready = sem("xw_hi_ready"), sem("v_hi_ready"), sem("ht_hi_ready")
        moments_ready, sd_ready, h_ready = sem("moments_ready"), sem("sd_ready"), sem("h_ready")
        moments2_ready, sd2_ready, o_ready = sem("moments2_ready"), sem("sd2_ready"), sem("o_ready")
        h_kept_ready, k_gauss_ready, relu_ready = sem("h_kept_ready"), sem("k_gauss_ready"), sem("relu_ready")
        ln_step, ln2_step = sem("ln_step"), sem("ln2_step")
        ht_split, ht_last_split = sem("ht_split"), sem("ht_last_split")
        grams_ready, p_ready, p_mirrored, g_ready = (sem("grams_ready"), sem("p_ready"),
                                                     sem("p_mirrored"), sem("g_ready"))
        diag_ready, sq_ready, guarded, rooted = (sem("diag_ready"), sem("sq_ready"), sem("guarded"),
                                                 sem("rooted"))
        d_ready, factors_spread, kern_ready = sem("d_ready"), sem("factors_spread"), sem("kern_ready")
        gauss_ready, masked_ready, k_ready = sem("gauss_ready"), sem("masked_ready"), sem("k_ready")
        kt_ready, kt_hi_ready, kt_split = sem("kt_ready"), sem("kt_hi_ready"), sem("kt_split")
        small_step, row_step = sem("small_step"), sem("row_step")
        SMALL, ROW = 6, 9

        def rows(g, b):
            return g * GROUP + (b + 1)

        def use_of(when, i, use):
            bank, before = ring_use(when, i, use)
            return banks[bank], ring_full[bank], ring_read[bank], before

        def f32(t):
            return t.bitcast(F32)

        with nc.Block() as block:
            @block.sync
            def _(sp):
                def load(g, b):
                    sp.dma_start(x_sb[:, b, :],
                                 x[bass.ds(g * GROUP + b, 1)].rearrange("a l n -> l (a n)")
                                 ).then_inc(x_in[b], 16)

                def x_used(when, i, b):
                    _, _, read, before = use_of(when, i, ("mix", b))
                    sp.wait_ge(read, before + 1)

                def store(i, b):
                    sp.wait_ge(o_ready, rows(i, b))
                    sp.dma_start(out[bass.ds(i * GROUP + b, 1)].rearrange("a l n -> l (a n)"),
                                 o_sb[:, b % 2, :]).then_inc(o_free[b % 2], 16)

                for b in range(GROUP):
                    load(0, b)
                for b in range(GROUP):
                    x_used("front", 0, b)
                    load(1, b)
                with sp.Fori(0, GROUPS - 2) as i:
                    for b in range(GROUP):
                        x_used("loop", i, b)
                        load(i + 2, b)
                    for b in range(GROUP):
                        store(i, b)
                for i in (GROUPS - 2, GROUPS - 1):
                    for b in range(GROUP):
                        store(i, b)
                for s in range(2):
                    sp.wait_ge(o_free[s], 16 * (1 + B // 2))

            @block.tensor
            def _(pe):
                def start_use(when, i, use):
                    bank, full, read, before = use_of(when, i, use)
                    if not (when == "front" and before == 0):
                        pe.wait_ge(read, before)
                    return bank, full

                def was_read(when, i, use):
                    _, _, read, before = use_of(when, i, use)
                    pe.wait_ge(read, before + 1)

                def split_product(out_ap, left, right, first, last):
                    (lh, ll), (rh, rl) = left, right
                    nc.tensor.matmul(out_ap, lh, rh, start=first, stop=False)
                    nc.tensor.matmul(out_ap, lh, rl, start=False, stop=False)
                    return nc.tensor.matmul(out_ap, ll, rh, start=False, stop=last)

                def xw(when, i, g, b):
                    bank, full = start_use(when, i, ("xw", b))
                    pe.wait_ge(x_in[b], (g + 1) * 16)
                    for t in range(NT):
                        last = nc.tensor.matmul(bank[:, tile_cols(t)], x_sb[:, b, tile_cols(t)], c["adj"][:],
                                                start=True, stop=True)
                    last.then_inc(full, 1)

                def mix(when, i, g, b):
                    bank, full = start_use(when, i, ("mix", b))
                    was_read(when, i, ("xw", b))
                    for t in range(NT):
                        last = split_product(bank[:], (xw_hi[:, b, t, :], xw_lo[:, b, t, :]),
                                             (an_hi[:, t, :], an_lo[:, t, :]), t == 0, t == NT - 1)
                    last.then_inc(full, 1)

                def h_transpose(when, i, g, b):
                    bank, full = start_use(when, i, ("h_t", b))
                    pe.wait_ge(h_ready, rows(g, b))
                    for t in range(NT):
                        last = nc.tensor.transpose(bank[:, tile_cols(t)], h[:, b, tile_cols(t)], c["ident"][:])
                    last.then_inc(full, 1)

                def t_products(when, i, m):
                    m_hi, m_lo = {"l": ml, "g": mg}[m]
                    pe.wait_ge(ht_split, i * (GROUP - 1) + (GROUP - 1))
                    pe.wait_ge(ht_last_split, i + 1)
                    for t in range(NT):
                        bank, full = start_use(when, i, ("t_" + m, t))
                        for j in range(t, NT):
                            last = split_product(bank[:], (m_hi[:, j, tile_cols(t)], m_lo[:, j, tile_cols(t)]),
                                                 (ht_hi[:, j, :, :], ht_lo[:, j, :, :]), j == t, j == NT - 1)
                        last.then_inc(full, 1)

                def grams(when, i, m):
                    was_read(when, i, ("t_" + m, NT - 1))
                    for b in range(GROUP):
                        for t in range(NT):
                            last = nc.tensor.matmul(gram_bank[m][:, tile_cols(b)], ht[:, t, b, :],
                                                    t_mat[m][:, t, b, :], start=(t == 0), stop=(t == NT - 1))
                    last.then_inc(grams_ready, 1)

                def values(when, i, b):
                    bank, full = start_use(when, i, ("v", b))
                    for t in range(NT):
                        last = split_product(bank[:], (ht_hi[:, t, b, :], ht_lo[:, t, b, :]),
                                             (vo[0][:, t, :], vo[1][:, t, :]), t == 0, t == NT - 1)
                    last.then_inc(full, 1)

                def mirror(i, m, n):
                    pe.wait_ge(p_ready, i * 2 + (n + 1))
                    for b in range(GROUP):
                        last = nc.tensor.transpose(mirror_bank[m][:, tile_cols(b)], p_mat[m][:, b, :],
                                                   c["ident"][:])
                    last.then_inc(p_mirrored, 1)

                def spread_factors(i, m, n):
                    pe.wait_ge(d_ready, i * 2 + (n + 1))
                    nc.tensor.matmul(spread_bank[m][:], c["ones_r"][:], flat(d_hi[m]), start=True, stop=False)
                    nc.tensor.matmul(spread_bank[m][:], c["ones_r"][:], flat(d_lo[m]), start=False, stop=True
                                     ).then_inc(factors_spread, 1)

                def k_transpose(i):
                    pe.wait_ge(k_ready, i + 1)
                    for b in range(GROUP):
                        last = nc.tensor.transpose(kt_bank[:, tile_cols(b)], k_mat[:, b, :], c["ident"][:])
                    last.then_inc(kt_ready, 1)

                def kv(when, i, b):
                    bank, full = start_use(when, i, ("kv", b))
                    if b == 0:
                        pe.wait_ge(kt_split, i + 1)
                        was_read(when, i, ("v", GROUP - 1))
                    split_product(bank[:], (kt_hi[:, b, :], kt_lo[:, b, :]), (v_hi[:, b, :], v_lo[:, b, :]),
                                  True, True).then_inc(full, 1)

                for step in (xw, mix, h_transpose):
                    for b in range(GROUP):
                        step("front", 0, 0, b)

                def group(when, i):
                    front = when == "loop"
                    t_products(when, i, "l")
                    t_products(when, i, "g")
                    grams(when, i, "l")
                    grams(when, i, "g")
                    values(when, i, 0)
                    values(when, i, 1)
                    mirror(i, "l", 0)
                    mirror(i, "g", 1)
                    values(when, i, 2)
                    values(when, i, 3)
                    if front:
                        for b in range(GROUP):
                            xw(when, i, i + 1, b)
                        mix(when, i, i + 1, 0)
                    spread_factors(i, "g", 0)
                    spread_factors(i, "l", 1)
                    if front:
                        for b in (1, 2, 3):
                            mix(when, i, i + 1, b)
                        for b in (0, 1):
                            h_transpose(when, i, i + 1, b)
                    k_transpose(i)
                    if front:
                        h_transpose(when, i, i + 1, 2)
                    kv(when, i, 0)
                    kv(when, i, 1)
                    if front:
                        h_transpose(when, i, i + 1, 3)
                    kv(when, i, 2)
                    kv(when, i, 3)

                with pe.Fori(0, GROUPS - 1) as i:
                    group("loop", i)
                group("back", GROUPS - 1)

            @block.scalar
            def _(act):
                def filled(when, i, use):
                    bank, full, read, before = use_of(when, i, use)
                    act.wait_ge(full, before + 1)
                    return bank, read

                def xw_high(when, i, b):
                    bank, _ = filled(when, i, ("xw", b))
                    nc.scalar.activation(xw_hi[:, b, :, :].rearrange("p t l -> p (t l)"), bank[:], ACT.Copy
                                         ).then_inc(xw_hi_ready, 1)

                def deviation(g, b):
                    act.wait_ge(moments_ready, rows(g, b))
                    nc.scalar.activation(sd[:, 0, b % 2, 0:1], moments[:, 0, b % 2, 1:2], ACT.Sqrt,
                                         bias=c["eps"][:]).then_inc(sd_ready, 1)

                def deviation2(i, b):
                    act.wait_ge(moments2_ready, rows(i, b))
                    nc.scalar.activation(sd[:, 1, b % 2, 0:1], moments[:, 1, b % 2, 1:2], ACT.Sqrt,
                                         bias=c["eps"][:]).then_inc(sd2_ready, 1)

                def copy_ht(when, i, b):
                    bank, read = filled(when, i, ("h_t", b))
                    nc.scalar.activation(ht[:, :, b, :], bank[:].rearrange("p (t n) -> p t n", t=NT),
                                         ACT.Copy).then_inc(read, 1)

                def copy_t(when, i, m, t):
                    bank, read = filled(when, i, ("t_" + m, t))
                    nc.scalar.activation(t_mat[m][:, t, :, :].rearrange("p b n -> p (b n)"), bank[:], ACT.Copy
                                         ).then_inc(read, 1)

                def copy_p(i, m, n):
                    act.wait_ge(grams_ready, i * 2 + (n + 1))
                    nc.scalar.activation(flat(p_mat[m]), gram_bank[m][:], ACT.Copy).then_inc(p_ready, 1)

                def v_high(when, i, b):
                    bank, _ = filled(when, i, ("v", b))
                    nc.scalar.activation(v_hi[:, b, :], bank[:], ACT.Copy).then_inc(v_hi_ready, 1)

                def norm_root(i):
                    act.wait_ge(guarded, i + 1)
                    nc.scalar.activation(norm[:, 1, :], norm[:, 0, :], ACT.Sqrt).then_inc(rooted, 1)

                def gauss(i):
                    act.wait_ge(kern_ready, i * 2 + 1)
                    for b in range(GROUP):
                        nc.scalar.activation(kern["g"][:, b, :], kern["g"][:, b, :], ACT.Relu,
                                             bias=sq["g"][:, b:b + 1]).then_inc(relu_ready, 1)
                    act.wait_ge(relu_ready, rows(i, GROUP - 1))
                    nc.scalar.activation(flat(kern["g"]), flat(kern["g"]), ACT.Exp, scale=scal[:, 2:3]
                                         ).then_inc(gauss_ready, 1)

                def kt_high(i):
                    act.wait_ge(kt_ready, i + 1)
                    nc.scalar.activation(flat(kt_hi), kt_bank[:], ACT.Copy).then_inc(kt_hi_ready, 1)

                for b in range(GROUP):
                    xw_high("front", 0, b)
                for b in range(GROUP):
                    deviation(0, b)
                for b in range(GROUP):
                    copy_ht("front", 0, b)

                def group(when, i):
                    front = when == "loop"
                    for m in "lg":
                        for t in range(NT):
                            copy_t(when, i, m, t)
                    copy_p(i, "l", 0)
                    copy_p(i, "g", 1)
                    for b in range(GROUP):
                        v_high(when, i, b)
                    if front:
                        xw_high(when, i, 0)
                        xw_high(when, i, 1)
                    norm_root(i)
                    if front:
                        xw_high(when, i, 2)
                        xw_high(when, i, 3)
                        deviation(i + 1, 0)
                    gauss(i)
                    if front:
                        for b in (1, 2, 3):
                            deviation(i + 1, b)
                        copy_ht(when, i, 0)
                        copy_ht(when, i, 1)
                    kt_high(i)
                    if front:
                        copy_ht(when, i, 2)
                    deviation2(i, 0)
                    deviation2(i, 1)
                    if front:
                        copy_ht(when, i, 3)
                    deviation2(i, 2)
                    deviation2(i, 3)

                with act.Fori(0, GROUPS - 1) as i:
                    group("loop", i)
                group("back", GROUPS - 1)

            @block.gpsimd
            def _(pool):
                def take_diagonal(i, m, n):
                    pool.wait_ge(g_ready, i * 2 + (n + 1))
                    nc.gpsimd.tensor_tensor(on_diag[m][:], g_mat[m][:], every_ident, ALU.mult
                                            ).then_inc(diag_ready, 1)

                def apply_mask(i, m, n):
                    if m == "l":
                        pool.wait_ge(kern_ready, i * 2 + 2)
                    else:
                        pool.wait_ge(gauss_ready, i + 1)
                    nc.gpsimd.tensor_tensor(masked[m][:], kern[m][:], every_mask, ALU.mult
                                            ).then_inc(masked_ready, 1)

                def ht_low(b, g):
                    pool.wait_ge(ht_hi_ready, rows(g, b))
                    nc.gpsimd.tensor_tensor(ht_lo[:, :, b, :], ht[:, :, b, :], f32(ht_hi[:, :, b, :]),
                                            ALU.subtract).then_inc(ht_split, 1)

                def keep_h(when, i, g, b):
                    pool.wait_ge(h_ready, rows(g, b))
                    if when == "loop":
                        _, _, read, before = use_of(when, i, ("kv", b))
                        pool.wait_ge(read, before + 1)
                    pool.nop(nofuse=True)
                    nc.gpsimd.tensor_scalar(h_kept[:, b, :], h[:, b, :], 1.0, 1.0, ALU.mult, ALU.mult
                                            ).then_inc(h_kept_ready, 1)

                for s in range(2):
                    nc.gpsimd.memset(o_sb[:, s, :], 0.0).then_inc(o_free[s], 16)
                for b in (0, 1, 2):
                    ht_low(b, 0)
                for b in range(GROUP):
                    keep_h("front", 0, 0, b)

                def group(when, i):
                    take_diagonal(i, "l", 0)
                    take_diagonal(i, "g", 1)
                    apply_mask(i, "l", 0)
                    apply_mask(i, "g", 1)
                    if when == "loop":
                        for b in (0, 1, 2):
                            ht_low(b, i + 1)
                        for b in range(GROUP):
                            keep_h(when, i, i + 1, b)

                with pool.Fori(0, GROUPS - 1) as i:
                    group("loop", i)
                group("back", GROUPS - 1)

            @block.vector
            def _(dve):
                def filled(when, i, use):
                    bank, full, read, before = use_of(when, i, use)
                    dve.wait_ge(full, before + 1)
                    return bank, read, before

                def v_low(when, i, b):
                    bank, _, read, _ = use_of(when, i, ("v", b))
                    dve.wait_ge(v_hi_ready, rows(i, b))
                    nc.vector.tensor_tensor(v_lo[:, b, :], bank[:], f32(v_hi[:, b, :]), ALU.subtract
                                            ).then_inc(read, 1)

                def xw_low(when, i, g, b):
                    bank, _, read, _ = use_of(when, i, ("xw", b))
                    dve.wait_ge(xw_hi_ready, rows(g, b))
                    nc.vector.tensor_tensor(xw_lo[:, b, :, :].rearrange("p t l -> p (t l)"), bank[:],
                                            f32(xw_hi[:, b, :, :]).rearrange("p t l -> p (t l)"),
                                            ALU.subtract).then_inc(read, 1)

                def layer0(when, i, g, b):
                    s = b % 2
                    bank, read, before = filled(when, i, ("mix", b))
                    nc.vector.scalar_tensor_tensor(out=y[:, s, :], in0=bank[:], scalar=c["bias"][:],
                                                   in1=x_sb[:, b, :], op0=ALU.add, op1=ALU.add
                                                   ).then_inc(read, 1)
                    dve.wait_ge(read, before + 1)
                    nc.vector.bn_stats(stats[:, 0, s, :], y[:, s, :]).then_inc(ln_step, 1)
                    dve.wait_ge(ln_step, g * 2 * GROUP + (2 * b + 1))
                    dve.nop(nofuse=True)
                    nc.vector.bn_aggr(moments[:, 0, s, :], stats[:, 0, s, :]).then_inc(moments_ready, 1)
                    dve.wait_ge(sd_ready, rows(g, b))
                    nc.vector.reciprocal(sd[:, 0, s, 1:2], sd[:, 0, s, 0:1]).then_inc(ln_step, 1)
                    dve.wait_ge(ln_step, g * 2 * GROUP + (2 * b + 2))
                    if when == "loop":
                        dve.wait_ge(h_kept_ready, rows(i, b))
                    nc.vector.tensor_scalar(h[:, b, :], y[:, s, :], moments[:, 0, s, 0:1], sd[:, 0, s, 1:2],
                                            ALU.subtract, ALU.mult).then_inc(h_ready, 1)

                def layer1(when, i, b):
                    s = b % 2
                    bank, read, before = filled(when, i, ("kv", b))
                    dve.wait_ge(h_kept_ready, rows(i, b))
                    nc.vector.tensor_tensor(y2[:, s, :], bank[:], h_kept[:, b, :], ALU.add).then_inc(read, 1)
                    dve.wait_ge(read, before + 1)
                    nc.vector.bn_stats(stats[:, 1, s, :], y2[:, s, :]).then_inc(ln2_step, 1)
                    dve.wait_ge(ln2_step, i * 2 * GROUP + (2 * b + 1))
                    dve.nop(nofuse=True)
                    nc.vector.bn_aggr(moments[:, 1, s, :], stats[:, 1, s, :]).then_inc(moments2_ready, 1)
                    dve.wait_ge(sd2_ready, rows(i, b))
                    nc.vector.reciprocal(sd[:, 1, s, 1:2], sd[:, 1, s, 0:1]).then_inc(ln2_step, 1)
                    dve.wait_ge(ln2_step, i * 2 * GROUP + (2 * b + 2))
                    dve.wait_ge(o_free[s], i * 32 + (b // 2 + 1) * 16)
                    nc.vector.tensor_scalar(o_sb[:, s, :], y2[:, s, :], moments[:, 1, s, 0:1],
                                            sd[:, 1, s, 1:2], ALU.subtract, ALU.mult).then_inc(o_ready, 1)

                def ht_high(when, i, g, b):
                    _, _, read, before = use_of(when, i, ("h_t", b))
                    dve.wait_ge(read, before + 1)
                    nc.vector.tensor_copy(ht_hi[:, :, b, :], ht[:, :, b, :]).then_inc(ht_hi_ready, 1)

                def ht_low_last(g):
                    dve.wait_ge(ht_hi_ready, rows(g, 3))
                    nc.vector.tensor_tensor(ht_lo[:, :, 3, :], ht[:, :, 3, :], f32(ht_hi[:, :, 3, :]),
                                            ALU.subtract).then_inc(ht_last_split, 1)

                def add_mirror(i, m, n):
                    dve.wait_ge(p_mirrored, i * 2 + (n + 1))
                    nc.vector.tensor_tensor(flat(g_mat[m]), flat(p_mat[m]), mirror_bank[m][:], ALU.add
                                            ).then_inc(g_ready, 1)

                def squares(i, m, n):
                    dve.wait_ge(diag_ready, i * 2 + (n + 1))
                    nc.vector.tensor_reduce(sq[m][:], on_diag[m][:], AX, ALU.add).then_inc(sq_ready, 1)

                def diagonals(i, m):
                    dve.wait_ge(small_step, i * SMALL + (2 if m == "g" else SMALL))
                    nc.vector.tensor_tensor(d_hi[m][:], every_ident, each(f32(small_hi[m][:])), ALU.mult)
                    nc.vector.tensor_tensor(d_lo[m][:], every_ident, each(f32(small_lo[m][:])), ALU.mult
                                            ).then_inc(d_ready, 1)

                def split_small(i, m, source, at):
                    nc.vector.tensor_copy(small_hi[m][:], source).then_inc(small_step, 1)
                    dve.wait_ge(small_step, i * SMALL + (at + 1))
                    nc.vector.tensor_tensor(small_lo[m][:], source, f32(small_hi[m][:]), ALU.subtract
                                            ).then_inc(small_step, 1)

                def square_factors(i):
                    squares(i, "l", 0)
                    dve.wait_ge(sq_ready, i * 2 + 1)
                    nc.vector.tensor_scalar(norm[:, 0, :], sq["l"][:], 0.0, None, ALU.max).then_inc(guarded, 1)
                    squares(i, "g", 1)
                    dve.wait_ge(sq_ready, i * 2 + 2)
                    split_small(i, "g", sq["g"][:], 0)
                    diagonals(i, "g")

                def norm_factors(i):
                    dve.wait_ge(rooted, i + 1)
                    nc.vector.tensor_scalar(norm[:, 1, :], norm[:, 1, :], KERNEL_EPS, None, ALU.max
                                            ).then_inc(small_step, 1)
                    dve.wait_ge(small_step, i * SMALL + 3)
                    nc.vector.reciprocal(norm[:, 2, :], norm[:, 1, :]).then_inc(small_step, 1)
                    dve.wait_ge(small_step, i * SMALL + 4)
                    split_small(i, "l", norm[:, 2, :], 4)
                    diagonals(i, "l")

                def kernels(i):
                    dve.wait_ge(factors_spread, i * 2 + 1)
                    nc.vector.scalar_tensor_tensor(out=flat(kern["g"]), in0=flat(g_mat["g"]), scalar=-2.0,
                                                   in1=spread_bank["g"][:], op0=ALU.mult, op1=ALU.add
                                                   ).then_inc(kern_ready, 1)
                    dve.wait_ge(factors_spread, i * 2 + 2)
                    nc.vector.scalar_tensor_tensor(out=flat(kern["l"]), in0=flat(g_mat["l"]), scalar=0.0,
                                                   in1=spread_bank["l"][:], op0=ALU.max, op1=ALU.mult
                                                   ).then_inc(kern_ready, 1)

                def stepped(i, n, ins):
                    ins.then_inc(row_step, 1)
                    dve.wait_ge(row_step, i * ROW + n)

                def combine(i):
                    r, q = row["l"], row["g"]
                    dve.wait_ge(masked_ready, i * 2 + 1)
                    stepped(i, 1, nc.vector.tensor_reduce(r[:, 0, :], masked["l"][:], AX, ALU.add))
                    stepped(i, 2, nc.vector.tensor_tensor(r[:, 1, :], r[:, 0, :], norm[:, 2, :], ALU.mult))
                    stepped(i, 3, nc.vector.tensor_scalar(r[:, 1, :], r[:, 1, :], KERNEL_EPS, None, ALU.max))
                    stepped(i, 4, nc.vector.reciprocal(r[:, 2, :], r[:, 1, :]))
                    stepped(i, 5, nc.vector.scalar_tensor_tensor(
                        out=r[:, 3, :], in0=r[:, 2, :], scalar=scal[:, 0:1], in1=norm[:, 2, :],
                        op0=ALU.mult, op1=ALU.mult))
                    dve.wait_ge(masked_ready, i * 2 + 2)
                    stepped(i, 6, nc.vector.tensor_reduce(q[:, 0, :], masked["g"][:], AX, ALU.add))
                    stepped(i, 7, nc.vector.tensor_scalar(q[:, 1, :], q[:, 0, :], KERNEL_EPS, None, ALU.max))
                    stepped(i, 8, nc.vector.reciprocal(q[:, 2, :], q[:, 1, :]))
                    stepped(i, 9, nc.vector.tensor_scalar(q[:, 3, :], q[:, 2, :], scal[:, 1:2], None, ALU.mult))
                    for b in range(GROUP):
                        nc.vector.tensor_scalar(k_mat[:, b, :], masked["g"][:, b, :], q[:, 3, b:b + 1], None,
                                                ALU.mult).then_inc(k_gauss_ready, 1)
                    for b in range(GROUP):
                        dve.wait_ge(k_gauss_ready, rows(i, b))
                        last = nc.vector.scalar_tensor_tensor(
                            out=k_mat[:, b, :], in0=masked["l"][:, b, :], scalar=r[:, 3, b:b + 1],
                            in1=k_mat[:, b, :], op0=ALU.mult, op1=ALU.add)
                    last.then_inc(k_ready, 1)

                def kt_low(i):
                    dve.wait_ge(kt_hi_ready, i + 1)
                    nc.vector.tensor_tensor(flat(kt_lo), kt_bank[:], f32(flat(kt_hi)), ALU.subtract
                                            ).then_inc(kt_split, 1)

                for b in range(GROUP):
                    xw_low("front", 0, 0, b)
                for b in range(GROUP):
                    layer0("front", 0, 0, b)
                for b in range(GROUP):
                    ht_high("front", 0, 0, b)
                ht_low_last(0)

                def group(when, i):
                    front = when == "loop"
                    v_low(when, i, 0)
                    v_low(when, i, 1)
                    add_mirror(i, "l", 0)
                    add_mirror(i, "g", 1)
                    v_low(when, i, 2)
                    v_low(when, i, 3)
                    square_factors(i)
                    if front:
                        xw_low(when, i, i + 1, 0)
                        xw_low(when, i, i + 1, 1)
                    norm_factors(i)
                    if front:
                        xw_low(when, i, i + 1, 2)
                        xw_low(when, i, i + 1, 3)
                        layer0(when, i, i + 1, 0)
                    kernels(i)
                    if front:
                        layer0(when, i, i + 1, 1)
                    combine(i)
                    if front:
                        layer0(when, i, i + 1, 2)
                        layer0(when, i, i + 1, 3)
                        ht_high(when, i, i + 1, 0)
                        ht_high(when, i, i + 1, 1)
                    kt_low(i)
                    if front:
                        ht_high(when, i, i + 1, 2)
                    layer1(when, i, 0)
                    layer1(when, i, 1)
                    if front:
                        ht_high(when, i, i + 1, 3)
                        ht_low_last(i + 1)
                    layer1(when, i, 2)
                    layer1(when, i, 3)

                with dve.Fori(0, GROUPS - 1) as i:
                    group("loop", i)
                group("back", GROUPS - 1)



INPUTS = ["x", "adj", "L0_gnn_bias", "L1_gnn_W_lang", "L1_gnn_W_grav", "L1_gnn_W_V", "L1_gnn_W_O",
          "L1_gnn_gate_logit", "L1_gnn_log_sigma"]


def kernel(**inputs):
    import numpy as np
    import concourse.bacc as bacc
    from concourse.bass_utils import run_bass_kernel_spmd

    nc = bacc.Bacc("TRN2", target_bir_lowering=False, num_devices=1)
    arrays, args = {}, []
    for name in INPUTS:
        a = np.ascontiguousarray(inputs[name])
        if a.ndim == 0:
            a = a.reshape(1, 1)
        arrays["in_" + name] = a
        args.append(nc.dram_tensor("in_" + name, a.shape, mybir.dt.from_np(a.dtype),
                                   kind="ExternalInput").ap())
    out = nc.dram_tensor("out", (B, L, N), F32, kind="ExternalOutput").ap()
    gated_graph_block(nc, *args, out)
    r = run_bass_kernel_spmd(nc, [arrays], core_ids=[0])
    return r.results[0]["out"]
```

```python
from contextlib import ExitStack

import concourse.bass as bass
from concourse import mybir

ALU = mybir.AluOpType
ACT = mybir.ActivationFunctionType
F32 = mybir.dt.float32
F32R = mybir.dt.float32r
AX = mybir.AxisListType.X

P = 128
B, L, N = 64, 128, 512
NT = N // P
TOPK = max(int(N * 0.3), 1)
ROUNDS = (TOPK + 7) // 8
DUMMIES = ROUNDS * 8 - TOPK
DUMMY, SELF, TAKEN = 1e30, -1e30, -3e38
NORM_EPS, KERNEL_EPS, LN_EPS = 1e-12, 1e-8, 1e-5
GROUP = 4
GROUPS = B // GROUP

CHUNK = 8
SLOTS = 2 * CHUNK
EARLY_ROWS = 4
LEAD = 13
PASSES = B // SLOTS
ROOTS_AT = SLOTS - LEAD
SIM_FROM = [0, P, 2 * P, 2 * P]


def tile_cols(t):
    return slice(t * P, (t + 1) * P)


def constants(nc, sb, sem, adj, bias, gate, log_sigma):
    c = {
        "ident": sb("ident", [P, P], F32),
        "ones": sb("ones", [P, P], F32),
        "ones_r": sb("ones_r", [P, P], F32R),
        "adj": sb("adj_sb", [P, P], F32),
        "mask": sb("mask", [P, P], F32),
        "bias": sb("bias_sb", [P, 1], F32),
        "gate": sb("gate_sb", [P, 1], F32),
        "log_sigma": sb("log_sigma_sb", [P, 1], F32),
        "scal": sb("scal", [P, 8], F32),
        "eps": sb("eps", [P, 1], F32),
    }
    return c


def gated_graph_block(nc, x, adj, bias, w_lang, w_grav, w_v, w_o, gate, log_sigma, out):
    with ExitStack() as whole:
        def sb(name, shape, dt, scope=whole):
            return scope.enter_context(nc.sbuf_tensor(name, shape, dt))

        def sem(name, scope=whole):
            return scope.enter_context(nc.semaphore(name))

        c = constants(nc, sb, sem, adj, bias, gate, log_sigma)
        banks = [whole.enter_context(nc.psum_tensor(f"bank{n}", [P, 512], F32)) for n in range(8)]
        an_hi = sb("an_hi", [P, NT, N], F32R)
        an_lo = sb("an_lo", [P, NT, N], F32R)
        kept = {"an": (an_hi, an_lo)}
        for name in ("ml", "mg", "vo"):
            kept[name] = (sb(name + "_hi", [P, NT, N], F32R), sb(name + "_lo", [P, NT, N], F32R))

        with ExitStack() as early:
            x_ring = sb("x_ring", [P, SLOTS, N], F32, early)
            x_in = [sem(f"x_in{s}") for s in range(SLOTS)]
            raw = {n: sb("raw_" + n, [P, NT, N], F32, early) for n in ("l", "g", "v", "o")}
            weights_in = sem("weights_in")
            setup_block(nc, sem, sb, early, c, x, x_ring, x_in, adj, bias, gate, log_sigma)
            similarity(nc, sb, sem, early, c, banks, x, x_ring, x_in, raw, weights_in,
                       {"l": w_lang, "g": w_grav, "v": w_v, "o": w_o})
            graph_and_weights(nc, sb, sem, early, c, banks, raw, weights_in, kept)
        layers(nc, sb, sem, c, banks, kept, x, out)



def setup_block(nc, sem, sb, early, c, x, x_ring, x_in, adj, bias, gate, log_sigma):
    small_in, filled, cleared = sem("small_in"), sem("filled"), sem("cleared")
    exps, step = sem("exps"), sem("setup_step")
    wide = sb("wide", [P, CHUNK + P], F32, early)
    c["place"] = sb("place", [P, CHUNK + P], F32R, early)
    c["pick"] = sb("pick", [P, CHUNK, P], F32R, early)
    both = sb("both", [P, CHUNK], F32, early)
    scal = c["scal"]

    with nc.Block() as block:
        @block.sync
        def _(sp):
            sp.dma_start(x_ring[:, 0, :], x[0]).then_inc(x_in[0], 16)
            sp.dma_start(c["adj"][:], adj).then_inc(small_in, 16)
            sp.dma_start(c["bias"][:], bias.rearrange("(p a) -> p a", a=1)).then_inc(small_in, 16)
            for name, source in (("gate", gate), ("log_sigma", log_sigma)):
                sp.dma_start(c[name][:], source.to_broadcast([P, 1])).then_inc(small_in, 16)
            for k in range(1, EARLY_ROWS):
                sp.dma_start(x_ring[:, k, :], x[k]).then_inc(x_in[k], 16)

        @block.gpsimd
        def _(pool):
            nc.gpsimd.memset(c["ident"][:], 0.0).then_inc(cleared, 1)
            nc.gpsimd.memset(wide[:], 0.0).then_inc(cleared, 1)
            nc.gpsimd.memset(c["ones"][:], 1.0).then_inc(filled, 1)
            nc.gpsimd.memset(c["eps"][:], LN_EPS).then_inc(filled, 1)
            pool.wait_ge(cleared, 2)
            nc.gpsimd.affine_select(out=c["ident"][:], in_=c["ident"][:], compare_op=ALU.not_equal,
                                    fill=1.0, base=0, pattern=[[-1, P]], channel_multiplier=1
                                    ).then_inc(filled, 1)
            nc.gpsimd.memset(wide[:, CHUNK - 1:CHUNK], 1.0).then_inc(filled, 1)
            nc.gpsimd.memset(wide[:, CHUNK + 63:CHUNK + 64], 1.0).then_inc(filled, 1)

        @block.scalar
        def _(act):
            act.wait_ge(small_in, 64)
            nc.scalar.activation(scal[:, 4:5], c["gate"][:], ACT.Exp, scale=-1.0).then_inc(exps, 1)
            nc.scalar.activation(scal[:, 5:6], c["log_sigma"][:], ACT.Exp).then_inc(exps, 1)

        @block.vector
        def _(dve):
            dve.wait_ge(filled, 5)
            nc.vector.tensor_copy(c["ones_r"][:], c["ones"][:])
            nc.vector.tensor_copy(c["place"][:], wide[:])
            nc.vector.tensor_tensor(both[:], c["ident"][:, 0:CHUNK], c["ident"][:, 64:64 + CHUNK],
                                    ALU.add).then_inc(step, 1)
            nc.vector.tensor_scalar(c["mask"][:], c["ident"][:], -1.0, 1.0, ALU.mult, ALU.add
                                    ).then_inc(step, 1)
            dve.wait_ge(step, 2)
            nc.vector.tensor_copy(c["pick"][:], both[:, :, None].to_broadcast([P, CHUNK, P]))
            dve.wait_ge(small_in, 64)
            nc.vector.tensor_tensor(c["mask"][:], c["mask"][:], c["adj"][:], ALU.mult).then_inc(step, 1)
            dve.wait_ge(exps, 2)
            nc.vector.tensor_scalar(scal[:, 6:7], scal[:, 4:5], 1.0, None, ALU.add).then_inc(step, 1)
            nc.vector.tensor_scalar(scal[:, 7:8], scal[:, 5:6], scal[:, 5:6], -2.0, ALU.mult, ALU.mult
                                    ).then_inc(step, 1)
            dve.wait_ge(step, 5)
            nc.vector.reciprocal(scal[:, 0:1], scal[:, 6:7]).then_inc(step, 1)
            nc.vector.reciprocal(scal[:, 2:3], scal[:, 7:8]).then_inc(step, 1)
            dve.wait_ge(step, 7)
            nc.vector.tensor_scalar(scal[:, 1:2], scal[:, 0:1], -1.0, 1.0, ALU.mult, ALU.add)



def similarity(nc, sb, sem, early, c, banks, x, x_ring, x_in, raw, weights_in, weights):
    with ExitStack() as scope:
        def buf(name, shape, dt):
            return sb(name, shape, dt, scope)

        sq = buf("sq", [P, 4, N], F32)
        sq_hi = buf("sq_hi", [P, 4, N], F32R)
        sq_lo = buf("sq_lo", [P, 4, N], F32R)
        root = buf("root", [P, N], F32)
        inv = buf("inv", [P, N], F32)
        inv_split = buf("inv_split", [P, 2, N], F32R)
        xn = buf("xn", [P, 4, N], F32)
        xn_hi = buf("xn_hi", [P, 4, N], F32R)
        xn_lo = buf("xn_lo", [P, 4, N], F32R)
        sums, spread = banks[4:6], banks[6:8]

        squared, squares_split, squares_used = sem("squared"), sem("squares_split"), sem("squares_used")
        roots_ready, clamped = sem("roots_ready"), sem("clamped")
        inverted, inv_hi_ready, inv_ready = sem("inverted"), sem("inv_hi_ready"), sem("inv_ready")
        spread_ready, scaled, hi_ready, lo_ready = (sem("spread_ready"), sem("scaled"), sem("hi_ready"),
                                                    sem("lo_ready"))
        grams_done = sem("grams_done")

        with nc.Block() as block:
            @block.sync
            def _(sp):
                for k in range(EARLY_ROWS, SLOTS):
                    sp.dma_start(x_ring[:, k, :], x[k]).then_inc(x_in[k], 16)
                with sp.Fori(0, PASSES - 1) as p:
                    for j in range(SLOTS):
                        sp.wait_ge(scaled, p * SLOTS + (j + 1))
                        sp.dma_start(x_ring[:, j, :],
                                     x[bass.ds(p * SLOTS + (SLOTS + j), 1)].rearrange("a l n -> l (a n)")
                                     ).then_inc(x_in[j], 16)
                for name in ("l", "g", "o", "v"):
                    sp.dma_start(raw[name][:], weights[name].rearrange("(t p) d -> p t d", p=P)
                                 ).then_inc(weights_in, 16)

            @block.gpsimd
            def _(pool):
                def split(p, j, first=False):
                    pool.wait_ge(squared, p * SLOTS + (j + 1))
                    if not (first and j < 4):
                        pool.wait_ge(squares_used, p * SLOTS + (j - 3))
                    nc.gpsimd.tensor_tensor(sq_lo[:, j % 4, :], sq[:, j % 4, :], sq_hi[:, j % 4, :].bitcast(F32),
                                            ALU.subtract).then_inc(squares_split, 1)

                for k in range(LEAD):
                    split(0, k, first=True)
                with pool.Fori(0, PASSES - 1) as p:
                    for j in range(SLOTS):
                        split(p, j + LEAD)
                for j in range(SLOTS - LEAD):
                    split(PASSES - 1, j + LEAD)

            @block.scalar
            def _(act):
                def square(p, j, first=False):
                    act.wait_ge(x_in[j % SLOTS], (p + (1 + j // SLOTS)) * 16)
                    if not (first and j < 4):
                        act.wait_ge(squares_split, p * SLOTS + (j - 3))
                        act.wait_ge(squares_used, p * SLOTS + (j - 3))
                    nc.scalar.activation(sq[:, j % 4, :], x_ring[:, j % SLOTS, :], ACT.Square)
                    nc.scalar.activation(sq_hi[:, j % 4, :], x_ring[:, j % SLOTS, :], ACT.Square
                                         ).then_inc(squared, 1)

                def roots(p, chunk, first=False):
                    act.wait_ge(squares_used, p * SLOTS + (chunk + 1) * CHUNK)
                    if not (first and chunk == 0):
                        act.wait_ge(inverted, p * 2 * NT + chunk * NT)
                    nc.scalar.activation(root[:], sums[chunk % 2][:], ACT.Sqrt).then_inc(roots_ready, 1)

                def hi(p, j, first=False):
                    act.wait_ge(scaled, p * SLOTS + (j + 1))
                    if not (first and j < 4):
                        act.wait_ge(grams_done, p * SLOTS + (j - 3))
                    nc.scalar.activation(xn_hi[:, j % 4, :], xn[:, j % 4, :], ACT.Copy).then_inc(hi_ready, 1)

                for k in range(LEAD):
                    square(0, k, first=True)
                    if k == CHUNK:
                        roots(0, 0, first=True)

                def one_pass(p, last=False, first=False):
                    for j in range(SLOTS):
                        if not last or j + LEAD < SLOTS:
                            square(p, j + LEAD)
                        if j == ROOTS_AT:
                            roots(p, 1)
                        if j == ROOTS_AT + CHUNK and not last:
                            roots(p, 2)
                        hi(p, j, first)

                one_pass(0, first=True)
                with act.Fori(1, PASSES - 1) as p:
                    one_pass(p)
                one_pass(PASSES - 1, last=True)

            @block.vector
            def _(dve):
                def clamp(p, chunk):
                    dve.wait_ge(roots_ready, p * 2 + (chunk + 1))
                    nc.vector.tensor_scalar(root[:], root[:], NORM_EPS, None, ALU.max).then_inc(clamped, 1)

                def invert(p, chunk, t):
                    if t == 0:
                        dve.wait_ge(clamped, p * 2 + (chunk + 1))
                    nc.vector.reciprocal(inv[:, tile_cols(t)], root[:, tile_cols(t)]).then_inc(inverted, 1)

                def split_inverse(p, chunk, first=False):
                    side = chunk % 2
                    dve.wait_ge(inverted, p * 2 * NT + (chunk + 1) * NT)
                    if not (first and chunk < 2):
                        dve.wait_ge(spread_ready, p * SLOTS + (chunk - 1) * CHUNK)
                    nc.vector.tensor_copy(inv_split[:, side, :], inv[:]).then_inc(inv_hi_ready, 1)
                    dve.wait_ge(inv_hi_ready, p * 2 + (chunk + 1))
                    nc.vector.tensor_tensor(inv_split[64:P, side, :], inv[64:P, :],
                                            inv_split[64:P, side, :].bitcast(F32), ALU.subtract).then_inc(inv_ready, 1)

                def scale(p, j, first=False):
                    if not (first and j < 4):
                        dve.wait_ge(lo_ready, p * SLOTS + (j - 3))
                    dve.wait_ge(spread_ready, p * SLOTS + (j + 1))
                    nc.vector.tensor_tensor(xn[:, j % 4, :], x_ring[:, j % SLOTS, :], spread[j % 2][:],
                                            ALU.mult).then_inc(scaled, 1)

                def lo(p, j, first=False):
                    dve.wait_ge(hi_ready, p * SLOTS + (j + 1))
                    nc.vector.tensor_tensor(xn_lo[:, j % 4, :], xn[:, j % 4, :], xn_hi[:, j % 4, :].bitcast(F32),
                                            ALU.subtract).then_inc(lo_ready, 1)

                clamp(0, 0)
                for t in range(NT):
                    invert(0, 0, t)
                split_inverse(0, 0, first=True)

                scale(0, 0, first=True)

                def one_pass(p, last=False, first=False):
                    for j in range(SLOTS):
                        if not last or j + 1 < SLOTS:
                            scale(p, j + 1, first)
                        lo(p, j)
                        for at, chunk in ((ROOTS_AT, 1), (ROOTS_AT + CHUNK, 2)):
                            if chunk == 2 and last:
                                continue
                            if j == at:
                                clamp(p, chunk)
                            if at <= j < at + 2:
                                invert(p, chunk, j - at)
                            if j == at + 2:
                                invert(p, chunk, 2)
                                invert(p, chunk, 3)
                                split_inverse(p, chunk, first)

                one_pass(0, first=True)
                with dve.Fori(1, PASSES - 1) as p:
                    one_pass(p)
                one_pass(PASSES - 1, last=True)

            @block.tensor
            def _(pe):
                def sum_squares(p, j, first=False):
                    side = banks[4 + (j // CHUNK) % 2]
                    b = j % CHUNK
                    where = c["place"][:, CHUNK - 1 - b:CHUNK - 1 - b + P]
                    pe.wait_ge(squares_split, p * SLOTS + (j + 1))
                    if b == 0 and not (first and j < SLOTS):
                        pe.wait_ge(roots_ready, p * 2 + (j // CHUNK - 1))
                    nc.tensor.matmul(side[:], where, sq_hi[:, j % 4, :], start=(b == 0), stop=False)
                    last = nc.tensor.matmul(side[:], where, sq_lo[:, j % 4, :], start=False,
                                            stop=(b == CHUNK - 1))
                    last.then_inc(squares_used, 1)
                    return last

                def spread_inverse(p, j, first=False):
                    if j % CHUNK == 0:
                        pe.wait_ge(inv_ready, p * 2 + (j // CHUNK + 1))
                    if not (first and j < 2):
                        pe.wait_ge(scaled, p * SLOTS + (j - 1))
                    nc.tensor.matmul(spread[j % 2][:], c["pick"][:, j % CHUNK, :],
                                     inv_split[:, (j // CHUNK) % 2, :], start=True, stop=True
                                     ).then_inc(spread_ready, 1)

                def gram(p, j, start=False, stop=False):
                    pe.wait_ge(lo_ready, p * SLOTS + (j + 1))
                    h, l = xn_hi[:, j % 4, :], xn_lo[:, j % 4, :]
                    for n, (left, right) in enumerate(((h, h), (h, l), (l, h))):
                        for t in range(NT):
                            last = nc.tensor.matmul(banks[t][:, 0:N - SIM_FROM[t]], left[:, tile_cols(t)],
                                                    right[:, SIM_FROM[t]:N], start=(start and n == 0),
                                                    stop=(stop and n == 2))
                    last.then_inc(grams_done, 1)

                for k in range(LEAD):
                    sum_squares(0, k, first=True)
                spread_inverse(0, 0, first=True)
                spread_inverse(0, 1, first=True)

                def one_pass(p, first=False, last=False):
                    for j in range(SLOTS):
                        if not last or j + LEAD < SLOTS:
                            sum_squares(p, j + LEAD, first)
                        if not last or j + 2 < SLOTS:
                            spread_inverse(p, j + 2, first)
                        gram(p, j, start=(first and j == 0), stop=(last and j == SLOTS - 1))

                one_pass(0, first=True)
                with pe.Fori(1, PASSES - 1) as p:
                    one_pass(p)
                one_pass(PASSES - 1, last=True)



def graph_and_weights(nc, sb, sem, early, c, banks, raw, weights_in, kept):
    with ExitStack() as scope:
        def buf(name, shape, dt):
            return sb(name, shape, dt, scope)

        sim = buf("sim", [P, NT, N], F32)
        work = buf("work", [P, NT, N + DUMMIES], F32)
        top8 = buf("top8", [P, NT, 8], F32)
        graph = buf("graph", [P, NT, N], F32)
        wo_t = buf("wo_t", [P, NT, N], F32)
        full = buf("full", [P, 2, N], F32)
        diag = buf("diag", [P, NT, P], F32)
        deg = buf("deg", [P, 5, NT], F32)
        an = buf("an", [P, 2, N], F32)
        an_hi, an_lo = kept["an"]
        degree_bank, mirror_banks, dinv_bank = banks[7], banks[4:7], banks[4]
        ident4 = c["ident"][:, None, :].to_broadcast([P, NT, P])

        sim_upper, mirrored, sim_ready = sem("sim_upper"), sem("mirrored"), sem("sim_ready")
        work_ready, top8_ready, graph_ready = sem("work_ready"), sem("top8_ready"), sem("graph_ready")
        product_ready, product_read, product_split = (sem("product_ready"), sem("product_read"),
                                                      sem("product_split"))
        degree_spread, degree_step, degree_root = sem("degree_spread"), sem("degree_step"), sem("degree_root")
        dinv_spread, an_ready, an_hi_ready, an_read = (sem("dinv_spread"), sem("an_ready"),
                                                       sem("an_hi_ready"), sem("an_read"))

        products = ([("ml", t) for t in range(NT)] + [("mg", t) for t in range(NT)]
                    + [("wo_t", t) for t in range(NT)] + [("vo", t) for t in range(NT)])
        width = {kind: [N] * NT for kind in ("wo_t", "vo")}
        width["ml"] = width["mg"] = [(t + 1) * P for t in range(NT)]
        split_products = [n for n, (kind, _) in enumerate(products) if kind != "wo_t"]

        with nc.Block() as block:
            @block.tensor
            def _(pe):
                for rows, bank in ((1, 0), (2, 1), (3, 2)):
                    pe.wait_ge(sim_upper, min(rows, 2))
                    for t in range(min(rows, 2)):
                        last = nc.tensor.transpose(mirror_banks[bank][:, tile_cols(t)],
                                                   sim[:, t, tile_cols(rows)], c["ident"][:])
                    last.then_inc(mirrored, 1)
                pe.wait_ge(weights_in, 64)
                pe.wait_ge(sim_upper, NT)
                for n, (kind, t) in enumerate(products):
                    bank = banks[n % 4]
                    if n >= 4:
                        pe.wait_ge(product_read, n - 3)
                    if (kind, t) == ("vo", 0):
                        pe.wait_ge(product_read, n)
                    for k in range(NT):
                        if kind == "wo_t":
                            last = nc.tensor.transpose(bank[:, tile_cols(k)], raw["o"][:, k, tile_cols(t)],
                                                       c["ident"][:])
                        elif kind == "vo":
                            last = nc.tensor.matmul(bank[:], raw["v"][:, k, tile_cols(t)], wo_t[:, k, :],
                                                    start=(k == 0), stop=(k == NT - 1))
                        else:
                            w = raw[kind[1]]
                            last = nc.tensor.matmul(bank[:, 0:width[kind][t]], w[:, k, tile_cols(t)],
                                                    w[:, k, 0:width[kind][t]], start=(k == 0),
                                                    stop=(k == NT - 1))
                    last.then_inc(product_ready, 1)
                for t in range(NT):
                    pe.wait_ge(graph_ready, t + 1)
                    last = nc.tensor.matmul(degree_bank[:], c["ones"][:], graph[:, t, :],
                                            start=(t == 0), stop=(t == NT - 1))
                last.then_inc(degree_spread, 1)
                pe.wait_ge(degree_step, 7)
                nc.tensor.matmul(dinv_bank[:], c["ones"][:], diag[:], start=True, stop=True
                                 ).then_inc(dinv_spread, 1)

            @block.scalar
            def _(act):
                for t in range(NT):
                    nc.scalar.activation(sim[:, t, SIM_FROM[t]:N], banks[t][:, 0:N - SIM_FROM[t]],
                                         ACT.Copy, scale=1.0 / B).then_inc(sim_upper, 1)
                for rows, bank in ((1, 0), (2, 1), (3, 2)):
                    act.wait_ge(mirrored, rows)
                    w = min(rows, 2) * P
                    nc.scalar.activation(sim[:, rows, 0:w], mirror_banks[bank][:, 0:w], ACT.Copy
                                         ).then_inc(sim_ready, 1)
                for n, (kind, t) in enumerate(products):
                    bank, w = banks[n % 4], width[kind][t]
                    act.wait_ge(product_ready, n + 1)
                    if kind == "wo_t":
                        nc.scalar.activation(wo_t[:, t, :], bank[:], ACT.Copy).then_inc(product_read, 1)
                        continue
                    m = split_products.index(n)
                    if m >= 2:
                        act.wait_ge(product_split, m - 1)
                    parts = [(0, w, 1.0)] if kind == "vo" else [(0, w - P, 1.0), (w - P, w, 0.5)]
                    for a, b, scale in parts:
                        if a == b:
                            continue
                        nc.scalar.activation(full[:, m % 2, a:b], bank[:, a:b], ACT.Copy, scale=scale)
                        last = nc.scalar.activation(kept[kind][0][:, t, a:b], bank[:, a:b], ACT.Copy,
                                                    scale=scale)
                    last.then_inc(product_read, 1)
                act.wait_ge(degree_step, 3)
                nc.scalar.activation(deg[:, 2, :], deg[:, 1, :], ACT.Sqrt).then_inc(degree_root, 1)
                for t in range(NT):
                    act.wait_ge(an_ready, t + 1)
                    nc.scalar.activation(an_hi[:, t, :], an[:, t % 2, :], ACT.Copy).then_inc(an_hi_ready, 1)

            @block.gpsimd
            def _(pool):
                for m, n in enumerate(split_products):
                    kind, t = products[n]
                    w = width[kind][t]
                    pool.wait_ge(product_read, n + 1)
                    nc.gpsimd.tensor_tensor(kept[kind][1][:, t, 0:w], full[:, m % 2, 0:w],
                                            kept[kind][0][:, t, 0:w].bitcast(F32), ALU.subtract
                                            ).then_inc(product_split, 1)

            @block.vector
            def _(dve):
                nc.vector.memset(work[:, :, N:N + DUMMIES], DUMMY)
                for t in range(NT):
                    if t == 0:
                        dve.wait_ge(sim_upper, 1)
                    else:
                        dve.wait_ge(sim_ready, t)
                    nc.vector.tensor_copy(work[:, t, 0:N], sim[:, t, :]).then_inc(top8_ready, 1)
                for t in range(NT):
                    dve.wait_ge(top8_ready, t + 1)
                    nc.vector.scalar_tensor_tensor(out=work[:, t, tile_cols(t)], in0=c["ident"][:],
                                                   scalar=SELF, in1=sim[:, t, tile_cols(t)],
                                                   op0=ALU.mult, op1=ALU.add).then_inc(work_ready, 1)
                with dve.Fori(0, ROUNDS) as r:
                    for t in range(NT):
                        dve.wait_ge(work_ready, r * NT + (t + 1))
                        dve.nop(nofuse=True)
                        nc.vector.max(top8[:, t, :], work[:, t, :]).then_inc(top8_ready, 1)
                    for t in range(NT):
                        dve.wait_ge(top8_ready, r * NT + (NT + t + 1))
                        dve.nop(nofuse=True)
                        nc.vector.match_replace(work[:, t, :], top8[:, t, :], work[:, t, :], TAKEN
                                                ).then_inc(work_ready, 1)
                for t in range(NT):
                    dve.wait_ge(work_ready, ROUNDS * NT + t + 1)
                    nc.vector.scalar_tensor_tensor(out=graph[:, t, :], in0=work[:, t, 0:N], scalar=TAKEN,
                                                   in1=sim[:, t, :], op0=ALU.is_equal, op1=ALU.mult
                                                   ).then_inc(graph_ready, 1)
                dve.wait_ge(degree_spread, 1)
                nc.vector.tensor_tensor(diag[:], degree_bank[:].rearrange("p (t m) -> p t m", t=NT),
                                        ident4, ALU.mult).then_inc(degree_step, 1)
                dve.wait_ge(degree_step, 1)
                nc.vector.tensor_reduce(deg[:, 0, :], diag[:], AX, ALU.add).then_inc(degree_step, 1)
                dve.wait_ge(degree_step, 2)
                nc.vector.tensor_scalar(deg[:, 1, :], deg[:, 0, :], 1.2e-38, None, ALU.max
                                        ).then_inc(degree_step, 1)
                nc.vector.tensor_scalar(deg[:, 3, :], deg[:, 0, :], 0.0, None, ALU.is_gt
                                        ).then_inc(degree_step, 1)
                dve.wait_ge(degree_root, 1)
                nc.vector.reciprocal(deg[:, 2, :], deg[:, 2, :]).then_inc(degree_step, 1)
                dve.wait_ge(degree_step, 5)
                nc.vector.tensor_tensor(deg[:, 4, :], deg[:, 2, :], deg[:, 3, :], ALU.mult
                                        ).then_inc(degree_step, 1)
                dve.wait_ge(degree_step, 6)
                nc.vector.tensor_tensor(diag[:], ident4, deg[:, 4, :, None].to_broadcast([P, NT, P]),
                                        ALU.mult).then_inc(degree_step, 1)
                dve.wait_ge(dinv_spread, 1)

                def split_an(t):
                    dve.wait_ge(an_hi_ready, t + 1)
                    nc.vector.tensor_tensor(an_lo[:, t, :], an[:, t % 2, :], an_hi[:, t, :].bitcast(F32), ALU.subtract
                                            ).then_inc(an_read, 1)

                for t in range(NT):
                    if t >= 2:
                        dve.wait_ge(an_read, t - 1)
                    nc.vector.scalar_tensor_tensor(out=an[:, t % 2, :], in0=graph[:, t, :],
                                                   scalar=deg[:, 4, t:t + 1], in1=dinv_bank[:],
                                                   op0=ALU.mult, op1=ALU.mult).then_inc(an_ready, 1)
                    if t:
                        split_an(t - 1)
                split_an(NT - 1)



PREV, SAME, NEXT, AFTER = -1, 0, 1, 2
VARIANTS = {"first": {"head", "front", "ahead"}, "loop": {"tail", "head", "front", "ahead"},
            "before_last": {"tail", "head", "front"}, "last": {"tail", "head"}, "end": {"tail"}}
BEFORE = {"first": "prologue", "loop": "loop", "before_last": "loop", "last": "before_last", "end": "last"}

RING = 6
DOWN = list(range(NT))[::-1]
BODY_USES = ([("head", "t_l", t, SAME) for t in DOWN]
             + [("head", "t_g", t, SAME) for t in DOWN]
             + [("tail", "kv", b, PREV) for b in range(GROUP)]
             + [("front", "mix", b, NEXT) for b in range(GROUP)]
             + [("head", "v", 0, SAME), ("head", "v", 1, SAME), ("front", "h_t", 0, NEXT),
                ("head", "v", 2, SAME), ("front", "h_t", 1, NEXT), ("front", "h_t", 2, NEXT),
                ("head", "v", 3, SAME), ("front", "h_t", 3, NEXT)]
             + [("ahead", "xw", b, AFTER) for b in range(GROUP)])
BANK_OF = {(kind, n): at % RING for at, (_, kind, n, _) in enumerate(BODY_USES)}
PROLOGUE_USES = ([("xw", b, NEXT) for b in range(GROUP)]
                 + [(kind, n, at) for part, kind, n, at in BODY_USES if part in ("front", "ahead")])


def uses_of(when):
    if when == "prologue":
        return PROLOGUE_USES
    return [(kind, n, at) for part, kind, n, at in BODY_USES if part in VARIANTS[when]]


def last_user(when, kind, n, at):
    mine = uses_of(when)
    for use in mine[:mine.index((kind, n, at))][::-1]:
        if BANK_OF[use[:2]] == BANK_OF[kind, n]:
            return use
    if when == "prologue":
        return None
    for k, m, place in uses_of(BEFORE[when])[::-1]:
        if BANK_OF[k, m] == BANK_OF[kind, n]:
            return k, m, place - 1


def layers(nc, sb, sem, c, banks, kept, x, out):
    with ExitStack() as scope:
        def buf(name, shape, dt):
            return sb(name, shape, dt, scope)

        x_sb = buf("x_sb", [P, GROUP, N], F32)
        xw_hi, xw_lo = (buf(n, [P, GROUP, NT, P], F32R) for n in ("xw_hi", "xw_lo"))
        y = buf("y", [P, 2, N], F32)
        h = buf("h", [P, GROUP, N], F32)
        h_kept = buf("h_kept", [P, GROUP, N], F32)
        ht = buf("ht", [P, NT, GROUP, P], F32)
        ht_hi, ht_lo = (buf(n, [P, NT, GROUP, P], F32R) for n in ("ht_hi", "ht_lo"))
        t_mat = {"l": buf("t_l", [P, NT, GROUP, P], F32), "g": buf("t_g", [P, NT, GROUP, P], F32)}
        v_hi, v_lo = (buf(n, [P, GROUP, N], F32R) for n in ("v_hi", "v_lo"))
        p_mat = {m: buf("p_" + m, [P, GROUP, P], F32) for m in "lg"}
        g_mat = {m: buf("g_" + m, [P, GROUP, P], F32) for m in "lg"}
        on_diag = {m: buf("on_diag_" + m, [P, GROUP, P], F32) for m in "lg"}
        d_hi = {m: buf("d_hi_" + m, [P, GROUP, P], F32R) for m in "lg"}
        d_lo = {m: buf("d_lo_" + m, [P, GROUP, P], F32R) for m in "lg"}
        kern = {m: buf("kern_" + m, [P, GROUP, P], F32) for m in "lg"}
        masked = {m: on_diag[m] for m in "lg"}
        k_mat = buf("k_mat", [P, GROUP, P], F32)
        kt_hi, kt_lo = (buf(n, [P, GROUP, P], F32R) for n in ("kt_hi", "kt_lo"))
        y2 = buf("y2", [P, 2, N], F32)
        o_sb = buf("o_sb", [P, 2, N], F32)
        stats = buf("stats", [P, 2, 2, 6], F32)
        moments = buf("moments", [P, 2, 2, 2], F32)
        sd = buf("sd", [P, 2, 2, 3], F32)
        sq = {m: buf("sq_" + m, [P, GROUP], F32) for m in "lg"}
        norm = buf("norm", [P, 3, GROUP], F32)
        small_hi = {m: buf("small_hi_" + m, [P, GROUP], F32R) for m in "lg"}
        small_lo = {m: buf("small_lo_" + m, [P, GROUP], F32R) for m in "lg"}
        row = {m: buf("row_" + m, [P, 4, GROUP], F32) for m in "lg"}
        (ml, mg, vo), (an_hi, an_lo) = (kept[n] for n in ("ml", "mg", "vo")), kept["an"]
        scal = c["scal"]
        every_ident = c["ident"][:, None, :].to_broadcast([P, GROUP, P])
        every_mask = c["mask"][:, None, :].to_broadcast([P, GROUP, P])

        def each(small):
            return small[:, :, None].to_broadcast([P, GROUP, P])

        def flat(t):
            return t[:].rearrange("p b m -> p (b m)")

        gram_bank = mirror_bank = spread_bank = {"l": banks[6], "g": banks[7]}
        kt_bank = banks[7]

        kinds = ("t_l", "t_g", "v", "kv", "xw", "mix", "h_t")
        full = {kind: sem("full_" + kind) for kind in kinds}
        read = {kind: sem("read_" + kind) for kind in kinds}
        x_in = [sem(f"xb_in{b}") for b in range(GROUP)]
        o_free = [sem(f"o_free{s}") for s in range(2)]
        xw_hi_ready, v_hi_ready, ht_hi_ready = sem("xw_hi_ready"), sem("v_hi_ready"), sem("ht_hi_ready")
        moments_ready, sd_ready, h_ready = sem("moments_ready"), sem("sd_ready"), sem("h_ready")
        moments2_ready, sd2_ready, o_ready = sem("moments2_ready"), sem("sd2_ready"), sem("o_ready")
        h_kept_ready, k_gauss_ready, relu_ready = sem("h_kept_ready"), sem("k_gauss_ready"), sem("relu_ready")
        stats_ready, stats2_ready = sem("stats_ready"), sem("stats2_ready")
        inverse_ready, inverse2_ready = sem("inverse_ready"), sem("inverse2_ready")
        ln_ready, ln2_ready = sem("ln_ready"), sem("ln2_ready")
        ht_split, ht_last_split = sem("ht_split"), sem("ht_last_split")
        grams_ready, p_ready, p_mirrored, g_ready = (sem("grams_ready"), sem("p_ready"),
                                                     sem("p_mirrored"), sem("g_ready"))
        diag_ready, sq_ready, guarded, rooted = (sem("diag_ready"), sem("sq_ready"), sem("guarded"),
                                                 sem("rooted"))
        d_ready, factors_spread, kern_ready = sem("d_ready"), sem("factors_spread"), sem("kern_ready")
        gauss_ready, masked_ready, k_ready = sem("gauss_ready"), sem("masked_ready"), sem("k_ready")
        kt_ready, kt_hi_ready, kt_split = sem("kt_ready"), sem("kt_hi_ready"), sem("kt_split")
        small_step, row_step = sem("small_step"), sem("row_step")
        SMALL, ROW = 6, 9

        def rows(g, b):
            return g * GROUP + (b + 1)

        def bank_of(kind, n):
            return banks[BANK_OF[kind, n]]

        def f32(t):
            return t.bitcast(F32)

        def run_bodies(engine, body):
            body("first", 0)
            with engine.Fori(1, GROUPS - 2) as i:
                body("loop", i)
            body("before_last", GROUPS - 2)
            body("last", GROUPS - 1)
            body("end", GROUPS)

        with nc.Block() as block:
            @block.sync
            def _(sp):
                def load(g, b):
                    sp.dma_start(x_sb[:, b, :],
                                 x[bass.ds(g * GROUP + b, 1)].rearrange("a l n -> l (a n)")
                                 ).then_inc(x_in[b], 16)

                def store(g, b):
                    sp.wait_ge(o_ready, rows(g, b) + 2)
                    sp.dma_start(out[bass.ds(g * GROUP + b, 1)].rearrange("a l n -> l (a n)"),
                                 o_sb[:, b % 2, :]).then_inc(o_free[b % 2], 16)

                for b in range(GROUP):
                    load(0, b)
                for b in range(GROUP):
                    sp.wait_ge(read["mix"], rows(0, b))
                    load(1, b)

                def body(when, i):
                    for b in range(GROUP):
                        if "tail" in VARIANTS[when]:
                            store(i - 1, b)
                    for b in range(GROUP):
                        if "ahead" in VARIANTS[when]:
                            sp.wait_ge(read["mix"], rows(i + 1, b))
                            load(i + 2, b)

                run_bodies(sp, body)
                for s in range(2):
                    sp.wait_ge(o_free[s], 16 * (1 + B // 2))

            @block.tensor
            def _(pe):
                def start(when, i, kind, n, at):
                    user = last_user(when, kind, n, at)
                    if user:
                        k, m, place = user
                        nth = NT - 1 - m if k in ("t_l", "t_g") else m
                        pe.wait_ge(read[k], rows(i + place, nth))
                    return bank_of(kind, n)

                def split_product(out_ap, left, right, first, last):
                    (lh, ll), (rh, rl) = left, right
                    nc.tensor.matmul(out_ap, lh, rh, start=first, stop=False)
                    nc.tensor.matmul(out_ap, lh, rl, start=False, stop=False)
                    return nc.tensor.matmul(out_ap, ll, rh, start=False, stop=last)

                def xw(when, i, b, at):
                    bank = start(when, i, "xw", b, at)
                    pe.wait_ge(x_in[b], (i + at + 1) * 16)
                    for t in range(NT):
                        last = nc.tensor.matmul(bank[:, tile_cols(t)], x_sb[:, b, tile_cols(t)], c["adj"][:],
                                                start=True, stop=True)
                    last.then_inc(full["xw"], 1)

                def mix(when, i, b):
                    bank = start(when, i, "mix", b, NEXT)
                    pe.wait_ge(read["xw"], rows(i + 1, b))
                    for t in range(NT):
                        last = split_product(bank[:], (xw_hi[:, b, t, :], xw_lo[:, b, t, :]),
                                             (an_hi[:, t, :], an_lo[:, t, :]), t == 0, t == NT - 1)
                    last.then_inc(full["mix"], 1)

                def h_transpose(when, i, b):
                    bank = start(when, i, "h_t", b, NEXT)
                    pe.wait_ge(h_ready, rows(i + 1, b))
                    for t in range(NT):
                        last = nc.tensor.transpose(bank[:, tile_cols(t)], h[:, b, tile_cols(t)], c["ident"][:])
                    last.then_inc(full["h_t"], 1)

                def t_product(when, i, m, t):
                    m_hi, m_lo = {"l": ml, "g": mg}[m]
                    bank = start(when, i, "t_" + m, t, SAME)
                    for j in range(t, NT):
                        last = split_product(bank[:], (m_hi[:, j, tile_cols(t)], m_lo[:, j, tile_cols(t)]),
                                             (ht_hi[:, j, :, :], ht_lo[:, j, :, :]), j == t, j == NT - 1)
                    last.then_inc(full["t_" + m], 1)

                def grams(i, m):
                    pe.wait_ge(read["t_" + m], rows(i, NT - 1))
                    for b in range(GROUP):
                        for t in range(NT):
                            last = nc.tensor.matmul(gram_bank[m][:, tile_cols(b)], ht[:, t, b, :],
                                                    t_mat[m][:, t, b, :], start=(t == 0), stop=(t == NT - 1))
                    last.then_inc(grams_ready, 1)

                def values(when, i, b):
                    bank = start(when, i, "v", b, SAME)
                    for t in range(NT):
                        last = split_product(bank[:], (ht_hi[:, t, b, :], ht_lo[:, t, b, :]),
                                             (vo[0][:, t, :], vo[1][:, t, :]), t == 0, t == NT - 1)
                    last.then_inc(full["v"], 1)

                def mirror(i, m, n):
                    pe.wait_ge(p_ready, i * 2 + (n + 1))
                    for b in range(GROUP):
                        last = nc.tensor.transpose(mirror_bank[m][:, tile_cols(b)], p_mat[m][:, b, :],
                                                   c["ident"][:])
                    last.then_inc(p_mirrored, 1)

                def spread_factors(i, m, n):
                    pe.wait_ge(d_ready, i * 2 + (n + 1))
                    nc.tensor.matmul(spread_bank[m][:], c["ones_r"][:], flat(d_hi[m]), start=True, stop=False)
                    nc.tensor.matmul(spread_bank[m][:], c["ones_r"][:], flat(d_lo[m]), start=False, stop=True
                                     ).then_inc(factors_spread, 1)

                def k_transpose(g):
                    pe.wait_ge(k_ready, g + 1)
                    for b in range(GROUP):
                        last = nc.tensor.transpose(kt_bank[:, tile_cols(b)], k_mat[:, b, :], c["ident"][:])
                    last.then_inc(kt_ready, 1)

                def kv(when, i, b):
                    bank = start(when, i, "kv", b, PREV)
                    if b == 0:
                        pe.wait_ge(kt_split, i)
                        pe.wait_ge(read["v"], rows(i - 1, GROUP - 1))
                    split_product(bank[:], (kt_hi[:, b, :], kt_lo[:, b, :]), (v_hi[:, b, :], v_lo[:, b, :]),
                                  True, True).then_inc(full["kv"], 1)

                for b in range(GROUP):
                    xw("prologue", -1, b, NEXT)
                for b in range(GROUP):
                    mix("prologue", -1, b)
                for b in range(GROUP):
                    h_transpose("prologue", -1, b)
                for b in range(GROUP):
                    xw("prologue", -1, b, AFTER)

                def body(when, i):
                    parts = VARIANTS[when]
                    if "head" in parts:
                        pe.wait_ge(ht_split, i * (GROUP - 1) + (GROUP - 1))
                        pe.wait_ge(ht_last_split, i + 1)
                        for t in DOWN:
                            t_product(when, i, "l", t)
                        for t in DOWN:
                            t_product(when, i, "g", t)
                    if "tail" in parts:
                        k_transpose(i - 1)
                    if "head" in parts:
                        grams(i, "l")
                    if "tail" in parts:
                        for b in range(GROUP):
                            kv(when, i, b)
                    if "head" in parts:
                        grams(i, "g")
                    if "front" in parts:
                        mix(when, i, 0)
                        mix(when, i, 1)
                    if "head" in parts:
                        mirror(i, "l", 0)
                        mirror(i, "g", 1)
                    if "front" in parts:
                        mix(when, i, 2)
                        mix(when, i, 3)
                    if "head" in parts:
                        values(when, i, 0)
                        values(when, i, 1)
                    if when == "last":
                        spread_factors(i, "g", 0)
                        spread_factors(i, "l", 1)
                    if "front" in parts:
                        h_transpose(when, i, 0)
                    if "head" in parts:
                        values(when, i, 2)
                    if "front" in parts:
                        h_transpose(when, i, 1)
                        h_transpose(when, i, 2)
                    if "head" in parts:
                        values(when, i, 3)
                    if "front" in parts:
                        h_transpose(when, i, 3)
                    if "ahead" in parts:
                        xw(when, i, 0, AFTER)
                        xw(when, i, 1, AFTER)
                    if "front" in parts:
                        spread_factors(i, "g", 0)
                        spread_factors(i, "l", 1)
                    if "ahead" in parts:
                        xw(when, i, 2, AFTER)
                        xw(when, i, 3, AFTER)

                run_bodies(pe, body)

            @block.scalar
            def _(act):
                def xw_high(g, b):
                    act.wait_ge(full["xw"], rows(g, b))
                    nc.scalar.activation(xw_hi[:, b, :, :].rearrange("p t l -> p (t l)"),
                                         bank_of("xw", b)[:], ACT.Copy).then_inc(xw_hi_ready, 1)

                def deviation(layer, g, b):
                    s = b % 2
                    act.wait_ge((moments_ready, moments2_ready)[layer], rows(g, b))
                    nc.scalar.activation(sd[:, layer, s, 0:1], moments[:, layer, s, 1:2], ACT.Sqrt,
                                         bias=c["eps"][:]).then_inc((sd_ready, sd2_ready)[layer], 1)

                def normalise(layer, g, b, first=False):
                    s = b % 2
                    act.wait_ge((ln_ready, ln2_ready)[layer], rows(g, b))
                    if layer == 0:
                        if not first:
                            act.wait_ge(h_kept_ready, rows(g - 1, b))
                        target, done, source = h[:, b, :], h_ready, y
                    else:
                        act.wait_ge(o_free[s], g * 32 + (b // 2 + 1) * 16)
                        target, done, source = o_sb[:, s, :], o_ready, y2
                    nc.scalar.activation(target, source[:, s, :], ACT.Identity, scale=sd[:, layer, s, 1:2],
                                         bias=sd[:, layer, s, 2:3]).then_inc(done, 1)

                def copy_ht(g, b):
                    act.wait_ge(full["h_t"], rows(g, b))
                    nc.scalar.activation(ht[:, :, b, :], bank_of("h_t", b)[:].rearrange("p (t n) -> p t n", t=NT),
                                         ACT.Copy).then_inc(read["h_t"], 1)

                def copy_t(i, m, t):
                    act.wait_ge(full["t_" + m], rows(i, NT - 1 - t))
                    nc.scalar.activation(t_mat[m][:, t, :, :].rearrange("p b n -> p (b n)"),
                                         bank_of("t_" + m, t)[:], ACT.Copy).then_inc(read["t_" + m], 1)

                def copy_p(i, m, n):
                    act.wait_ge(grams_ready, i * 2 + (n + 1))
                    nc.scalar.activation(flat(p_mat[m]), gram_bank[m][:], ACT.Copy).then_inc(p_ready, 1)

                def v_high(i, b):
                    act.wait_ge(full["v"], rows(i, b))
                    nc.scalar.activation(v_hi[:, b, :], bank_of("v", b)[:], ACT.Copy).then_inc(v_hi_ready, 1)

                def norm_root(i):
                    act.wait_ge(guarded, i + 1)
                    nc.scalar.activation(norm[:, 1, :], norm[:, 0, :], ACT.Sqrt).then_inc(rooted, 1)

                def gauss(g):
                    act.wait_ge(kern_ready, g * 2 + 1)
                    for b in range(GROUP):
                        nc.scalar.activation(kern["g"][:, b, :], kern["g"][:, b, :], ACT.Relu,
                                             bias=sq["g"][:, b:b + 1]).then_inc(relu_ready, 1)
                    act.wait_ge(relu_ready, rows(g, GROUP - 1))
                    nc.scalar.activation(flat(kern["g"]), flat(kern["g"]), ACT.Exp, scale=scal[:, 2:3]
                                         ).then_inc(gauss_ready, 1)

                def kt_high(g):
                    act.wait_ge(kt_ready, g + 1)
                    nc.scalar.activation(flat(kt_hi), kt_bank[:], ACT.Copy).then_inc(kt_hi_ready, 1)

                for b in range(GROUP):
                    xw_high(0, b)
                deviation(0, 0, 0)
                for b in range(GROUP):
                    if b + 1 < GROUP:
                        deviation(0, 0, b + 1)
                    normalise(0, 0, b, first=True)
                for b in range(GROUP):
                    copy_ht(0, b)
                for b in range(GROUP):
                    xw_high(1, b)

                def body(when, i):
                    parts = VARIANTS[when]
                    if "tail" in parts:
                        gauss(i - 1)
                    if "head" in parts:
                        for m in "lg":
                            for t in DOWN:
                                copy_t(i, m, t)
                    if "tail" in parts:
                        kt_high(i - 1)
                    if "head" in parts:
                        copy_p(i, "l", 0)
                    if "tail" in parts:
                        deviation(1, i - 1, 0)
                        deviation(1, i - 1, 1)
                        normalise(1, i - 1, 0)
                        deviation(1, i - 1, 2)
                        normalise(1, i - 1, 1)
                    if "head" in parts:
                        copy_p(i, "g", 1)
                    if "tail" in parts:
                        deviation(1, i - 1, 3)
                        normalise(1, i - 1, 2)
                        normalise(1, i - 1, 3)
                    if "front" in parts:
                        deviation(0, i + 1, 0)
                        deviation(0, i + 1, 1)
                        normalise(0, i + 1, 0)
                        normalise(0, i + 1, 1)
                        deviation(0, i + 1, 2)
                    if "head" in parts:
                        norm_root(i)
                    if "front" in parts:
                        normalise(0, i + 1, 2)
                        deviation(0, i + 1, 3)
                        normalise(0, i + 1, 3)
                    if "head" in parts:
                        v_high(i, 0)
                        v_high(i, 1)
                    if "front" in parts:
                        copy_ht(i + 1, 0)
                    if "head" in parts:
                        v_high(i, 2)
                    if "front" in parts:
                        copy_ht(i + 1, 1)
                        copy_ht(i + 1, 2)
                    if "head" in parts:
                        v_high(i, 3)
                    if "front" in parts:
                        copy_ht(i + 1, 3)
                    if "ahead" in parts:
                        for b in range(GROUP):
                            xw_high(i + 2, b)

                run_bodies(act, body)

            @block.gpsimd
            def _(pool):
                def take_diagonal(i, m, n):
                    pool.wait_ge(g_ready, i * 2 + (n + 1))
                    nc.gpsimd.tensor_tensor(on_diag[m][:], g_mat[m][:], every_ident, ALU.mult
                                            ).then_inc(diag_ready, 1)

                def apply_mask(g, m):
                    if m == "l":
                        pool.wait_ge(kern_ready, g * 2 + 2)
                    else:
                        pool.wait_ge(gauss_ready, g + 1)
                    nc.gpsimd.tensor_tensor(masked[m][:], kern[m][:], every_mask, ALU.mult
                                            ).then_inc(masked_ready, 1)

                def ht_low(g, b):
                    pool.wait_ge(ht_hi_ready, rows(g, b))
                    nc.gpsimd.tensor_tensor(ht_lo[:, :, b, :], ht[:, :, b, :], f32(ht_hi[:, :, b, :]),
                                            ALU.subtract).then_inc(ht_split, 1)

                def keep_h(i, b, tail):
                    pool.wait_ge(h_ready, rows(i, b))
                    if tail:
                        pool.wait_ge(read["kv"], rows(i - 1, b))
                    pool.nop(nofuse=True)
                    nc.gpsimd.tensor_scalar(h_kept[:, b, :], h[:, b, :], 1.0, 1.0, ALU.mult, ALU.mult
                                            ).then_inc(h_kept_ready, 1)

                for s in range(2):
                    nc.gpsimd.memset(o_sb[:, s, :], 0.0).then_inc(o_free[s], 16)
                    nc.gpsimd.memset(y2[:, s, :], 0.0).then_inc(o_ready, 1)
                for b in (0, 1, 2):
                    ht_low(0, b)

                def body(when, i):
                    parts = VARIANTS[when]
                    if "tail" in parts:
                        apply_mask(i - 1, "l")
                        apply_mask(i - 1, "g")
                    if "head" in parts:
                        for b in range(GROUP):
                            keep_h(i, b, "tail" in parts)
                        take_diagonal(i, "l", 0)
                        take_diagonal(i, "g", 1)
                    if "front" in parts:
                        for b in (0, 1, 2):
                            ht_low(i + 1, b)

                run_bodies(pool, body)

            @block.vector
            def _(dve):
                def v_low(i, b):
                    dve.wait_ge(v_hi_ready, rows(i, b))
                    nc.vector.tensor_tensor(v_lo[:, b, :], bank_of("v", b)[:], f32(v_hi[:, b, :]),
                                            ALU.subtract).then_inc(read["v"], 1)

                def xw_low(g, b):
                    dve.wait_ge(xw_hi_ready, rows(g, b))
                    nc.vector.tensor_tensor(xw_lo[:, b, :, :].rearrange("p t l -> p (t l)"), bank_of("xw", b)[:],
                                            f32(xw_hi[:, b, :, :]).rearrange("p t l -> p (t l)"),
                                            ALU.subtract).then_inc(read["xw"], 1)

                def residual(layer, g, b, first=False):
                    s = b % 2
                    if layer == 0:
                        dve.wait_ge(full["mix"], rows(g, b))
                        if not (first and b < 2):
                            dve.wait_ge(h_ready, rows(g, b) - 2)
                        nc.vector.scalar_tensor_tensor(out=y[:, s, :], in0=bank_of("mix", b)[:],
                                                       scalar=c["bias"][:], in1=x_sb[:, b, :],
                                                       op0=ALU.add, op1=ALU.add).then_inc(read["mix"], 1)
                        dve.wait_ge(read["mix"], rows(g, b))
                    else:
                        dve.wait_ge(full["kv"], rows(g, b))
                        dve.wait_ge(h_kept_ready, rows(g, b))
                        dve.wait_ge(o_ready, rows(g, b))
                        nc.vector.tensor_tensor(y2[:, s, :], bank_of("kv", b)[:], h_kept[:, b, :], ALU.add
                                                ).then_inc(read["kv"], 1)
                        dve.wait_ge(read["kv"], rows(g, b))
                    source, counted = ((y, stats_ready), (y2, stats2_ready))[layer]
                    nc.vector.bn_stats(stats[:, layer, s, :], source[:, s, :]).then_inc(counted, 1)
                    dve.wait_ge(counted, rows(g, b))
                    dve.nop(nofuse=True)
                    nc.vector.bn_aggr(moments[:, layer, s, :], stats[:, layer, s, :]
                                      ).then_inc((moments_ready, moments2_ready)[layer], 1)

                def inverse(layer, g, b):
                    s = b % 2
                    dve.wait_ge((sd_ready, sd2_ready)[layer], rows(g, b))
                    counted = (inverse_ready, inverse2_ready)[layer]
                    nc.vector.reciprocal(sd[:, layer, s, 1:2], sd[:, layer, s, 0:1]).then_inc(counted, 1)
                    dve.wait_ge(counted, rows(g, b))
                    nc.vector.scalar_tensor_tensor(out=sd[:, layer, s, 2:3], in0=moments[:, layer, s, 0:1],
                                                   scalar=-1.0, in1=sd[:, layer, s, 1:2], op0=ALU.mult,
                                                   op1=ALU.mult).then_inc((ln_ready, ln2_ready)[layer], 1)

                def ht_high(g, b):
                    dve.wait_ge(read["h_t"], rows(g, b))
                    nc.vector.tensor_copy(ht_hi[:, :, b, :], ht[:, :, b, :]).then_inc(ht_hi_ready, 1)

                def ht_low_last(g):
                    dve.wait_ge(ht_hi_ready, rows(g, 3))
                    nc.vector.tensor_tensor(ht_lo[:, :, 3, :], ht[:, :, 3, :], f32(ht_hi[:, :, 3, :]),
                                            ALU.subtract).then_inc(ht_last_split, 1)

                def add_mirror(i, m, n):
                    dve.wait_ge(p_mirrored, i * 2 + (n + 1))
                    nc.vector.tensor_tensor(flat(g_mat[m]), flat(p_mat[m]), mirror_bank[m][:], ALU.add
                                            ).then_inc(g_ready, 1)

                def squares(i, m, n):
                    dve.wait_ge(diag_ready, i * 2 + (n + 1))
                    nc.vector.tensor_reduce(sq[m][:], on_diag[m][:], AX, ALU.add).then_inc(sq_ready, 1)

                def diagonals(i, m):
                    dve.wait_ge(small_step, i * SMALL + (2 if m == "g" else SMALL))
                    nc.vector.tensor_tensor(d_hi[m][:], every_ident, each(f32(small_hi[m][:])), ALU.mult)
                    nc.vector.tensor_tensor(d_lo[m][:], every_ident, each(f32(small_lo[m][:])), ALU.mult
                                            ).then_inc(d_ready, 1)

                def split_small(i, m, source, at):
                    nc.vector.tensor_copy(small_hi[m][:], source).then_inc(small_step, 1)
                    dve.wait_ge(small_step, i * SMALL + (at + 1))
                    nc.vector.tensor_tensor(small_lo[m][:], source, f32(small_hi[m][:]), ALU.subtract
                                            ).then_inc(small_step, 1)

                def guarded_squares(i):
                    squares(i, "l", 0)
                    dve.wait_ge(sq_ready, i * 2 + 1)
                    nc.vector.tensor_scalar(norm[:, 0, :], sq["l"][:], 0.0, None, ALU.max).then_inc(guarded, 1)

                def square_factors(i):
                    squares(i, "g", 1)
                    dve.wait_ge(sq_ready, i * 2 + 2)
                    split_small(i, "g", sq["g"][:], 0)
                    diagonals(i, "g")

                def norm_factors(i):
                    dve.wait_ge(rooted, i + 1)
                    nc.vector.tensor_scalar(norm[:, 1, :], norm[:, 1, :], KERNEL_EPS, None, ALU.max
                                            ).then_inc(small_step, 1)
                    dve.wait_ge(small_step, i * SMALL + 3)
                    nc.vector.reciprocal(norm[:, 2, :], norm[:, 1, :]).then_inc(small_step, 1)
                    dve.wait_ge(small_step, i * SMALL + 4)
                    split_small(i, "l", norm[:, 2, :], 4)
                    diagonals(i, "l")

                def kernels(g):
                    dve.wait_ge(factors_spread, g * 2 + 1)
                    nc.vector.scalar_tensor_tensor(out=flat(kern["g"]), in0=flat(g_mat["g"]), scalar=-2.0,
                                                   in1=spread_bank["g"][:], op0=ALU.mult, op1=ALU.add
                                                   ).then_inc(kern_ready, 1)
                    dve.wait_ge(factors_spread, g * 2 + 2)
                    nc.vector.scalar_tensor_tensor(out=flat(kern["l"]), in0=flat(g_mat["l"]), scalar=0.0,
                                                   in1=spread_bank["l"][:], op0=ALU.max, op1=ALU.mult
                                                   ).then_inc(kern_ready, 1)

                def stepped(g, n, ins):
                    ins.then_inc(row_step, 1)
                    dve.wait_ge(row_step, g * ROW + n)

                def combine(g):
                    r, q = row["l"], row["g"]
                    dve.wait_ge(masked_ready, g * 2 + 1)
                    stepped(g, 1, nc.vector.tensor_reduce(r[:, 0, :], masked["l"][:], AX, ALU.add))
                    stepped(g, 2, nc.vector.tensor_tensor(r[:, 1, :], r[:, 0, :], norm[:, 2, :], ALU.mult))
                    stepped(g, 3, nc.vector.tensor_scalar(r[:, 1, :], r[:, 1, :], KERNEL_EPS, None, ALU.max))
                    stepped(g, 4, nc.vector.reciprocal(r[:, 2, :], r[:, 1, :]))
                    stepped(g, 5, nc.vector.scalar_tensor_tensor(
                        out=r[:, 3, :], in0=r[:, 2, :], scalar=scal[:, 0:1], in1=norm[:, 2, :],
                        op0=ALU.mult, op1=ALU.mult))
                    dve.wait_ge(masked_ready, g * 2 + 2)
                    stepped(g, 6, nc.vector.tensor_reduce(q[:, 0, :], masked["g"][:], AX, ALU.add))
                    stepped(g, 7, nc.vector.tensor_scalar(q[:, 1, :], q[:, 0, :], KERNEL_EPS, None, ALU.max))
                    stepped(g, 8, nc.vector.reciprocal(q[:, 2, :], q[:, 1, :]))
                    stepped(g, 9, nc.vector.tensor_scalar(q[:, 3, :], q[:, 2, :], scal[:, 1:2], None, ALU.mult))
                    for b in range(GROUP):
                        nc.vector.tensor_scalar(k_mat[:, b, :], masked["g"][:, b, :], q[:, 3, b:b + 1], None,
                                                ALU.mult).then_inc(k_gauss_ready, 1)
                    for b in range(GROUP):
                        dve.wait_ge(k_gauss_ready, rows(g, b))
                        last = nc.vector.scalar_tensor_tensor(
                            out=k_mat[:, b, :], in0=masked["l"][:, b, :], scalar=r[:, 3, b:b + 1],
                            in1=k_mat[:, b, :], op0=ALU.mult, op1=ALU.add)
                    last.then_inc(k_ready, 1)

                def kt_low(g):
                    dve.wait_ge(kt_hi_ready, g + 1)
                    nc.vector.tensor_tensor(flat(kt_lo), kt_bank[:], f32(flat(kt_hi)), ALU.subtract
                                            ).then_inc(kt_split, 1)

                for b in range(GROUP):
                    xw_low(0, b)
                for b in range(GROUP):
                    residual(0, 0, b, first=True)
                    if b:
                        inverse(0, 0, b - 1)
                inverse(0, 0, GROUP - 1)
                for b in range(GROUP):
                    ht_high(0, b)
                ht_low_last(0)
                for b in range(GROUP):
                    xw_low(1, b)

                def body(when, i):
                    parts = VARIANTS[when]
                    if "tail" in parts:
                        combine(i - 1)
                        kt_low(i - 1)
                        residual(1, i - 1, 0)
                        residual(1, i - 1, 1)
                        inverse(1, i - 1, 0)
                        residual(1, i - 1, 2)
                        inverse(1, i - 1, 1)
                        residual(1, i - 1, 3)
                        inverse(1, i - 1, 2)
                        inverse(1, i - 1, 3)
                    if "front" in parts:
                        residual(0, i + 1, 0)
                        residual(0, i + 1, 1)
                        inverse(0, i + 1, 0)
                    if "head" in parts:
                        add_mirror(i, "l", 0)
                        add_mirror(i, "g", 1)
                    if "front" in parts:
                        inverse(0, i + 1, 1)
                        residual(0, i + 1, 2)
                    if "head" in parts:
                        guarded_squares(i)
                    if "front" in parts:
                        inverse(0, i + 1, 2)
                        residual(0, i + 1, 3)
                    if "head" in parts:
                        square_factors(i)
                    if "front" in parts:
                        inverse(0, i + 1, 3)
                    if "head" in parts:
                        norm_factors(i)
                        v_low(i, 0)
                        v_low(i, 1)
                    if when == "last":
                        kernels(i)
                    if "front" in parts:
                        ht_high(i + 1, 0)
                    if "head" in parts:
                        v_low(i, 2)
                    if "front" in parts:
                        ht_high(i + 1, 1)
                        ht_high(i + 1, 2)
                    if "head" in parts:
                        v_low(i, 3)
                    if "front" in parts:
                        ht_high(i + 1, 3)
                        ht_low_last(i + 1)
                    if "ahead" in parts:
                        xw_low(i + 2, 0)
                        xw_low(i + 2, 1)
                    if "front" in parts:
                        kernels(i)
                    if "ahead" in parts:
                        xw_low(i + 2, 2)
                        xw_low(i + 2, 3)

                run_bodies(dve, body)



INPUTS = ["x", "adj", "L0_gnn_bias", "L1_gnn_W_lang", "L1_gnn_W_grav", "L1_gnn_W_V", "L1_gnn_W_O",
          "L1_gnn_gate_logit", "L1_gnn_log_sigma"]


def kernel(**inputs):
    import numpy as np
    import concourse.bacc as bacc
    from concourse.bass_utils import run_bass_kernel_spmd

    nc = bacc.Bacc("TRN2", target_bir_lowering=False, num_devices=1)
    arrays, args = {}, []
    for name in INPUTS:
        a = np.ascontiguousarray(inputs[name])
        if a.ndim == 0:
            a = a.reshape(1, 1)
        arrays["in_" + name] = a
        args.append(nc.dram_tensor("in_" + name, a.shape, mybir.dt.from_np(a.dtype),
                                   kind="ExternalInput").ap())
    out = nc.dram_tensor("out", (B, L, N), F32, kind="ExternalOutput").ap()
    gated_graph_block(nc, *args, out)
    r = run_bass_kernel_spmd(nc, [arrays], core_ids=[0])
    return r.results[0]["out"]
```
